# Optimizing a Trainium2 kernel written in Bass

```python
import numpy as np
import jax
import jax.numpy as jnp

def _softmax(x, axis=-1):
    return jax.nn.softmax(x, axis=axis)

def _gelu(x):
    return jax.nn.gelu(x, approximate=True)

def _silu(x):
    return jax.nn.silu(x)

def _sigmoid(x):
    return jax.nn.sigmoid(x)

def _layernorm(x, axis=-1, eps=1e-05):
    m = jnp.mean(x, axis=axis, keepdims=True)
    v = jnp.var(x, axis=axis, keepdims=True)
    return (x - m) / jnp.sqrt(v + eps)

def _scatter_add(tgt, idx, src, axis=0):
    return tgt.at[idx].add(src)

def _segment_sum(src, seg, n):
    return jax.ops.segment_sum(src, seg, n)
kernel_name = 'mk_lm_tower_d1_tok_ids512_r4_480511'

def setup_inputs(seed: int=0):
    np.random.seed(seed)
    _w = jnp.asarray

    def _rec_inputs():
        import jax
        import jax.numpy as jnp
        _rk = jax.random.key(seed)
        x = jax.random.randint(jax.random.fold_in(_rk, 1), (32, 512), 0, 64, jnp.int32)
        return x
    x = _rec_inputs()

    def _L0_tok_setup():
        import jax, jax.numpy as jnp
        import numpy as np
        NGRAM_SIZES = (2, 3, 4)
        HASH_VOCAB = 25000
        EMBED_DIM = 128
        BATCH, SEQ = (8, 1024)

        def _ngram_hash_ids(byte_sequence, n):
            L = byte_sequence.shape[1] - n + 1
            h = jnp.zeros((byte_sequence.shape[0], L), dtype=jnp.int64)
            for j in range(n):
                h = (h * 64 + byte_sequence[:, j:j + L]) % HASH_VOCAB
            return h

        def _ngram_embed(byte_sequence, table, n):
            B, S = byte_sequence.shape
            ids = _ngram_hash_ids(byte_sequence, n)
            emb = table[ids]
            out = jnp.zeros((B, S, table.shape[1]), dtype=table.dtype)
            c = n // 2
            return out.at[:, c:c + emb.shape[1]].set(emb)
        key = jax.random.key(seed)
        ks = jax.random.split(key, 6)
        return {'byte_sequence': jax.random.randint(ks[0], (BATCH, SEQ), 0, 64, dtype=jnp.int64), 'emb_2': jax.random.normal(ks[1], (HASH_VOCAB, EMBED_DIM), dtype=jnp.float32), 'emb_3': jax.random.normal(ks[2], (HASH_VOCAB, EMBED_DIM), dtype=jnp.float32), 'emb_4': jax.random.normal(ks[3], (HASH_VOCAB, EMBED_DIM), dtype=jnp.float32), 'proj_w': jax.random.normal(ks[4], (EMBED_DIM, len(NGRAM_SIZES) * EMBED_DIM), dtype=jnp.float32) * 0.02, 'proj_b': jax.random.normal(ks[5], (EMBED_DIM,), dtype=jnp.float32) * 0.02}
    _L0_tok_all = _L0_tok_setup()
    _L0_tok_in = {k: v for k, v in _L0_tok_all.items() if k in ('emb_2', 'emb_3', 'emb_4', 'proj_w', 'proj_b')}
    del _L0_tok_all

    def _L0_attn_setup():
        import jax, jax.numpy as jnp
        import numpy as np
        B, T, C, NB = (4, 1024, 128, 64)
        key = jax.random.key(seed)
        ks = jax.random.split(key, 6)
        s = 0.02
        return {'x': jax.random.normal(ks[0], (B, T, C), dtype=jnp.float32), 'basis': jax.random.normal(ks[1], (C, 2 * NB), dtype=jnp.float32), 'q_coeffs': jax.random.normal(ks[2], (C, 2 * NB), dtype=jnp.float32) * s, 'k_coeffs': jax.random.normal(ks[3], (C, 2 * NB), dtype=jnp.float32) * s, 'v_coeffs': jax.random.normal(ks[4], (C, 2 * NB), dtype=jnp.float32) * s, 'o_coeffs': jax.random.normal(ks[5], (C, 2 * NB), dtype=jnp.float32) * s, 'decay_logit': jnp.float32(3.0), 'out_scale': jnp.float32(0.1)}
    _L0_attn_all = _L0_attn_setup()
    _L0_attn_in = {k: v for k, v in _L0_attn_all.items() if k in ('basis', 'q_coeffs', 'k_coeffs', 'v_coeffs', 'o_coeffs', 'decay_logit', 'out_scale')}
    del _L0_attn_all

    def _L0_ffn_setup():
        import jax, jax.numpy as jnp
        import numpy as np
        DIM = 128
        INTER = 64
        SHARED_INTER = 256
        N_EXPERTS = 64
        TOP_K = 6
        key = jax.random.key(seed)
        ks = jax.random.split(key, 8)
        s = 0.05
        return {'x': jax.random.normal(ks[0], (2, 128, DIM), jnp.float32), 'w_gate': jax.random.normal(ks[1], (N_EXPERTS, DIM), jnp.float32) * s, 'w1': jax.random.normal(ks[2], (N_EXPERTS, INTER, DIM), jnp.float32) * s, 'w2': jax.random.normal(ks[3], (N_EXPERTS, INTER, DIM), jnp.float32) * s, 'w3': jax.random.normal(ks[4], (N_EXPERTS, INTER, DIM), jnp.float32) * s, 'w_sg': jax.random.normal(ks[5], (SHARED_INTER, DIM), jnp.float32) * s, 'w_su': jax.random.normal(ks[6], (SHARED_INTER, DIM), jnp.float32) * s, 'w_sd': jax.random.normal(ks[7], (DIM, SHARED_INTER), jnp.float32) * s}
    _L0_ffn_all = _L0_ffn_setup()
    _L0_ffn_in = {k: v for k, v in _L0_ffn_all.items() if k in ('w_gate', 'w1', 'w2', 'w3', 'w_sg', 'w_su', 'w_sd')}
    del _L0_ffn_all
    return {'x': x, 'L0_tok_emb_2': _L0_tok_in['emb_2'], 'L0_tok_emb_3': _L0_tok_in['emb_3'], 'L0_tok_emb_4': _L0_tok_in['emb_4'], 'L0_tok_proj_w': _L0_tok_in['proj_w'], 'L0_tok_proj_b': _L0_tok_in['proj_b'], 'L0_attn_basis': _L0_attn_in['basis'], 'L0_attn_q_coeffs': _L0_attn_in['q_coeffs'], 'L0_attn_k_coeffs': _L0_attn_in['k_coeffs'], 'L0_attn_v_coeffs': _L0_attn_in['v_coeffs'], 'L0_attn_o_coeffs': _L0_attn_in['o_coeffs'], 'L0_attn_decay_logit': _L0_attn_in['decay_logit'], 'L0_attn_out_scale': _L0_attn_in['out_scale'], 'L0_ffn_w_gate': _L0_ffn_in['w_gate'], 'L0_ffn_w1': _L0_ffn_in['w1'], 'L0_ffn_w2': _L0_ffn_in['w2'], 'L0_ffn_w3': _L0_ffn_in['w3'], 'L0_ffn_w_sg': _L0_ffn_in['w_sg'], 'L0_ffn_w_su': _L0_ffn_in['w_su'], 'L0_ffn_w_sd': _L0_ffn_in['w_sd']}

def reference(x, L0_tok_emb_2, L0_tok_emb_3, L0_tok_emb_4, L0_tok_proj_w, L0_tok_proj_b, L0_attn_basis, L0_attn_q_coeffs, L0_attn_k_coeffs, L0_attn_v_coeffs, L0_attn_o_coeffs, L0_attn_decay_logit, L0_attn_out_scale, L0_ffn_w_gate, L0_ffn_w1, L0_ffn_w2, L0_ffn_w3, L0_ffn_w_sg, L0_ffn_w_su, L0_ffn_w_sd):
    import jax
    import jax.numpy as jnp

    def _L0_tok_ref(byte_sequence, emb_2, emb_3, emb_4, proj_w, proj_b):
        import jax, jax.numpy as jnp
        import numpy as np
        NGRAM_SIZES = (2, 3, 4)
        HASH_VOCAB = 25000
        EMBED_DIM = 128
        BATCH, SEQ = (8, 1024)

        def _ngram_hash_ids(byte_sequence, n):
            L = byte_sequence.shape[1] - n + 1
            h = jnp.zeros((byte_sequence.shape[0], L), dtype=jnp.int64)
            for j in range(n):
                h = (h * 64 + byte_sequence[:, j:j + L]) % HASH_VOCAB
            return h

        def _ngram_embed(byte_sequence, table, n):
            B, S = byte_sequence.shape
            ids = _ngram_hash_ids(byte_sequence, n)
            emb = table[ids]
            out = jnp.zeros((B, S, table.shape[1]), dtype=table.dtype)
            c = n // 2
            return out.at[:, c:c + emb.shape[1]].set(emb)
        tables = (emb_2, emb_3, emb_4)
        combined = jnp.concatenate([_ngram_embed(byte_sequence, t, n) for t, n in zip(tables, NGRAM_SIZES)], axis=-1)
        return jnp.einsum('bsk,dk->bsd', combined, proj_w) + proj_b

    def _L0_attn_ref(x, basis, q_coeffs, k_coeffs, v_coeffs, o_coeffs, decay_logit, out_scale):
        import jax, jax.numpy as jnp
        import numpy as np
        B, T, C, NB = (4, 1024, 128, 64)
        dtype = x.dtype
        q_w = (basis @ q_coeffs.T).astype(dtype)
        k_w = (basis @ k_coeffs.T).astype(dtype)
        v_w = (basis @ v_coeffs.T).astype(dtype)
        o_w = (basis @ o_coeffs.T).astype(dtype)
        queries = x @ q_w
        keys = x @ k_w
        values = x @ v_w
        scores = jnp.einsum('btc,bsc->bts', queries, keys)
        decay = jax.nn.sigmoid(decay_logit)
        pos = jnp.arange(x.shape[1])
        diff = pos[None, :] - pos[:, None]
        expo = jnp.maximum(diff - 1, 0).astype(dtype)
        weights = jnp.where(diff > 0, jnp.power(decay.astype(dtype), expo), jnp.zeros((), dtype))
        scores = scores * weights[None, :, :]
        retrieved = jnp.einsum('bts,bsc->btc', scores, values)
        return retrieved @ o_w.T * out_scale.astype(dtype)

    def _L0_ffn_ref(x, w_gate, w1, w2, w3, w_sg, w_su, w_sd):
        import jax, jax.numpy as jnp
        import numpy as np
        DIM = 128
        INTER = 64
        SHARED_INTER = 256
        N_EXPERTS = 64
        TOP_K = 6
        orig_shape = x.shape
        xf = x.reshape(-1, x.shape[-1])
        T = xf.shape[0]
        scores = xf @ w_gate.T
        top_vals, top_idx = jax.lax.top_k(scores, TOP_K)
        expert_weights = jax.nn.softmax(top_vals, axis=-1)
        comb = jnp.zeros(scores.shape, xf.dtype).at[jnp.arange(T)[:, None], top_idx].set(expert_weights)
        x1 = jax.nn.silu(jnp.einsum('td,eid->tei', xf, w1))
        x3 = jnp.einsum('td,eid->tei', xf, w3)
        y = jnp.einsum('tei,eid->ted', x1 * x3, w2)
        routed = jnp.einsum('ted,te->td', y, comb)
        shared = jax.nn.silu(xf @ w_sg.T) * (xf @ w_su.T) @ w_sd.T
        return (routed + shared).reshape(orig_shape)
    h = _L0_tok_ref(x, L0_tok_emb_2, L0_tok_emb_3, L0_tok_emb_4, L0_tok_proj_w, L0_tok_proj_b)
    h = h + _L0_attn_ref(_layernorm(h, axis=-1), L0_attn_basis, L0_attn_q_coeffs, L0_attn_k_coeffs, L0_attn_v_coeffs, L0_attn_o_coeffs, L0_attn_decay_logit, L0_attn_out_scale)
    h = h + _L0_ffn_ref(_layernorm(h, axis=-1), L0_ffn_w_gate, L0_ffn_w1, L0_ffn_w2, L0_ffn_w3, L0_ffn_w_sg, L0_ffn_w_su, L0_ffn_w_sd)
    return h

_drawn_inputs = setup_inputs


def setup_inputs(seed=0):
    import zlib

    import numpy as np

    out = dict(_drawn_inputs(seed))
    spreads = {}
    factors = {'L0_ffn_w_gate': 8.0,
     'L0_ffn_w1': 8.0,
     'L0_ffn_w2': 8.0,
     'L0_ffn_w3': 8.0,
     'L0_ffn_w_sg': 8.0,
     'L0_ffn_w_su': 8.0,
     'L0_ffn_w_sd': 8.0}
    for name, (base, spread) in spreads.items():
        noise = np.random.default_rng([zlib.crc32(name.encode()), seed]).standard_normal(out[name].shape)
        drawn = base * np.exp(spread * noise) if base else spread * noise
        out[name] = jnp.asarray(drawn.astype(out[name].dtype))
    for name, factor in factors.items():
        out[name] = (out[name] * factor).astype(out[name].dtype)
    return out
```

```python
from contextlib import ExitStack

import concourse.bass as bass
import numpy as np
from concourse import mybir

ALU = mybir.AluOpType
ACT = mybir.ActivationFunctionType
AX_X = mybir.AxisListType.X
F32 = mybir.dt.float32
F32R = mybir.dt.float32r
I32 = mybir.dt.int32
U32 = mybir.dt.uint32

P = 128
SEQS, SEQ_LEN = 32, 512
CHUNKS = SEQ_LEN // P
VOCAB, BASE = 25000, 64.0
NGRAMS = 3
EXPERTS, INTER, TOP_K = 64, 64, 6
ROUTED = EXPERTS * INTER // P
SHARED = 256 // P
TILES = ROUTED + SHARED
BLOCK = 12
LEAD = 3
EPS = 1e-5
HUGE = 3e38
E_NUMBER = float(np.e)

VALID = [(1, SEQ_LEN), (1, SEQ_LEN - 1), (2, SEQ_LEN - 1)]

EMBED_T = (0, 1, 2)
EMBED_P = 4
XNT_1 = 7
KEYED = 9
SCORE = 11
STATE = 12
RETRIEVE = 14
PROJECT = 16
XNT_2 = 19
ROUTE = 21
COMB_T = 27
INDEX = 4
GATHER = 5


def hbuf_of(q):
    return 3 if q == TILES - 1 else q % 3


def build(nc, x, emb, proj_t, rows, basis_t, coeff_t, wg_t, up_gate, up_lin, down, out):
    ctx = ExitStack()
    with ctx:
        def sb(name, shape, dt=F32):
            return ctx.enter_context(nc.sbuf_tensor(name, shape, dt))

        def pb(name, shape, dt=F32):
            return ctx.enter_context(nc.psum_tensor(name, shape, dt))

        def sem(name):
            return ctx.enter_context(nc.semaphore(name))

        up_hi = sb("up_hi", [P, 2, TILES * P], F32R)
        up_lo = sb("up_lo", [P, 2, TILES * P], F32R)
        down_hi = sb("down_hi", [P, TILES * P], F32R)
        down_lo = sb("down_lo", [P, TILES * P], F32R)
        pick = sb("pick", [P, ROUTED * P], F32R)
        proj = sb("proj", [P, NGRAMS, P])
        wg = sb("wg", [P, EXPERTS])
        qk_w = sb("qk_w", [P, P])
        vo_w = sb("vo_w", [P, P])
        ident = sb("ident", [P, P])
        bias = sb("bias", [P, P])
        decay_mask = sb("decay_mask", [P, P])
        decay_out = sb("decay_out", [P, P])
        decay_in = sb("decay_in", [P, 1])
        decay_chunk = sb("decay_chunk", [P, 1])
        decay = sb("decay", [P, 1])
        scale = sb("scale", [P, 1])
        minus_half = sb("minus_half", [P, CHUNKS])
        ids = sb("ids", [P, NGRAMS, (SEQS + 2) * CHUNKS], U32)

        row = sb("row", [1, P + 2])
        ones_row = sb("ones_row", [1, P])
        xi = sb("xi", [P, P + 3], I32)
        tmp_i = sb("tmp_i", [P, P + 3], I32)
        dcol = sb("dcol", [P, 4])

        idx = sb("idx", [P, NGRAMS * CHUNKS], U32)
        gath = sb("gath", [P, NGRAMS, CHUNKS, P])
        emb_t = sb("emb_t", [P, NGRAMS, SEQ_LEN])
        h1 = sb("h1", [P, CHUNKS, P])
        stats = sb("stats", [P, CHUNKS, 6])
        moments = sb("moments", [P, CHUNKS, 2])
        var_eps = sb("var_eps", [P, CHUNKS])
        rstd = sb("rstd", [P, CHUNKS])
        xn = sb("xn", [P, CHUNKS, P])
        xn_t = sb("xn_t", [P, SEQ_LEN])
        keyed_t = sb("keyed_t", [P, SEQ_LEN])
        keyed_out = sb("keyed_out", [P, CHUNKS - 1, P])
        xn_in = sb("xn_in", [P, CHUNKS - 1, P])
        scores = sb("scores", [P, CHUNKS, P])
        state = sb("state", [P, CHUNKS - 1, P])
        logits = sb("logits", [P, CHUNKS, EXPERTS])
        top = sb("top", [P, CHUNKS, 8])
        struck = sb("struck", [P, CHUNKS, EXPERTS])
        expo = sb("expo", [P, CHUNKS, EXPERTS])
        total = sb("total", [P, CHUNKS])
        inv_total = sb("inv_total", [P, CHUNKS])
        comb = sb("comb", [P, CHUNKS, 2, EXPERTS], F32R)

        h2 = sb("h2", [P, 2, SEQ_LEN])
        x_hi = sb("x_hi", [P, 2, SEQ_LEN], F32R)
        x_lo = sb("x_lo", [P, 2, SEQ_LEN], F32R)
        comb_t = sb("comb_t", [P, 2, SEQ_LEN], F32R)

        work = sb("work", [P, 8 * SEQ_LEN])
        gate = work[:, 0:2 * SEQ_LEN].rearrange("p (a t) -> p a t", a=2)
        product = work[:, 2 * SEQ_LEN:4 * SEQ_LEN].rearrange("p (a t) -> p a t", a=2)
        hid = work[:, 4 * SEQ_LEN:6 * SEQ_LEN].rearrange("p (a t) -> p a t", a=2)
        y_t = work[:, 6 * SEQ_LEN:7 * SEQ_LEN]
        result = work[:, 7 * SEQ_LEN:8 * SEQ_LEN].rearrange("p (c d) -> p c d", c=CHUNKS)
        hid_hi = sb("hid_hi", [P, 4, SEQ_LEN], F32R)
        hid_lo = sb("hid_lo", [P, 4, SEQ_LEN], F32R)

        ps_gate = pb("ps_gate", [P, 2, SEQ_LEN])
        ps_lin = pb("ps_lin", [P, 2, SEQ_LEN])
        ps_comb = pb("ps_comb", [P, SEQ_LEN])
        ps_y = pb("ps_y", [P, SEQ_LEN])
        ps_a = pb("ps_a", [P, SEQ_LEN])
        ps_b = pb("ps_b", [P, SEQ_LEN])

        def chunked(t):
            return t[:, :].rearrange("p (c n) -> p c n", c=CHUNKS)

        stage = work[:, 0:2 * BLOCK * P].rearrange("p (a n) -> p a n", a=2)
        small_w = stage[:, 0, 0:5 * P].rearrange("p (a b) -> p a b", a=5)
        w_t = stage[:, 0, 5 * P:9 * P].rearrange("p (a b) -> p a b", a=4)
        W = P + 3
        xf = work[:, 2 * BLOCK * P:2 * BLOCK * P + 4 * W].rearrange("p (a t) -> p a t", a=4)
        tmp_f = work[:, 2 * BLOCK * P + 4 * W:2 * BLOCK * P + 7 * W].rearrange("p (a t) -> p a t", a=3)
        id_f = h1[:, 0:NGRAMS, :]
        power = h2[:, 0, 0:2 * P].rearrange("p (a b) -> p a b", a=2)
        zeros = gath[:, 0:2, :, :].rearrange("p n c d -> p (n c d)").rearrange("p (j m) -> p j m", m=INTER)
        half_pick = emb_t[:, 0:2, :].rearrange("p n t -> p (n t)").rearrange("p (j m) -> p j m", m=INTER)

        s_xi = sem("s_xi")
        s_x = sem("s_x")
        s_small = sem("s_small")
        s_row = sem("s_row")
        s_stage = [sem("s_stage0"), sem("s_stage1")]
        s_split_hi = sem("s_split_hi")
        s_split_lo = sem("s_split_lo")
        s_const = sem("s_const")
        s_ident = sem("s_ident")
        s_pow = sem("s_pow")
        s_spread_ps = sem("s_spread_ps")
        s_spread = sem("s_spread")
        s_decay = sem("s_decay")
        s_hash = sem("s_hash")
        s_hash_ps = sem("s_hash_ps")
        s_ids = sem("s_ids")
        s_wt_ps = sem("s_wt_ps")
        s_wt = sem("s_wt")
        s_av_ps = sem("s_av_ps")
        s_av = sem("s_av")
        steps = {e: sem("steps_" + e) for e in ("pool", "act", "sp")}
        s_idx = sem("s_idx")
        s_gath = sem("s_gath")
        s_emb_ps = sem("s_emb_ps")
        s_emb_act = sem("s_emb_act")
        s_emb_dve = sem("s_emb_dve")
        s_h1_ps = sem("s_h1_ps")
        s_mom = sem("s_mom")
        s_var = sem("s_var")
        s_rstd = sem("s_rstd")
        s_xn = sem("s_xn")
        s_xn_in = sem("s_xn_in")
        s_xnt1_ps = sem("s_xnt1_ps")
        s_xnt1 = sem("s_xnt1")
        s_key_ps = sem("s_key_ps")
        s_key = sem("s_key")
        s_key_out = sem("s_key_out")
        s_score_ps = sem("s_score_ps")
        s_score = sem("s_score")
        s_state_ps = sem("s_state_ps")
        s_state = sem("s_state")
        s_got_ps = sem("s_got_ps")
        s_got = sem("s_got")
        s_h2_ps = sem("s_h2_ps")
        s_xnt2_ps = sem("s_xnt2_ps")
        s_xnt2 = sem("s_xnt2")
        s_x_hi = sem("s_x_hi")
        s_x_lo = sem("s_x_lo")
        s_route_ps = sem("s_route_ps")
        s_logits = sem("s_logits")
        s_shift = sem("s_shift")
        s_exp = sem("s_exp")
        s_comb = sem("s_comb")
        s_combt_ps = sem("s_combt_ps")
        s_combt = sem("s_combt")
        s_y_free = sem("s_y_free")
        s_res_ps = sem("s_res_ps")
        s_res = sem("s_res")
        s_out = sem("s_out")
        s_room = sem("s_room")
        s_gate_ps = sem("s_gate_ps")
        s_lin_ps = sem("s_lin_ps")
        s_comb_ps = sem("s_comb_ps")
        s_gate = sem("s_gate")
        s_product = sem("s_product")
        s_hid = sem("s_hid")
        s_hid_hi = sem("s_hid_hi")
        s_hid_lo = sem("s_hid_lo")
        s_down = sem("s_down")

        block = ctx.enter_context(nc.Block())

        blocks = []
        for first in range(0, TILES, BLOCK):
            cols = slice(first * P, min(first + BLOCK, TILES) * P)
            for k, src in enumerate((up_gate, up_lin)):
                blocks.append((up_hi[:, k, cols], up_lo[:, k, cols], src[:, cols]))
            blocks.append((down_hi[:, cols], down_lo[:, cols], down[:, cols]))

        GATHERS = NGRAMS * CHUNKS

        def tile_of(p):
            return (p + LEAD) // TILES, (p + LEAD) % TILES


        @block.sync
        def _(sp):
            sp.dma_start(row[:, :], rows).then_inc(s_row, 16)
            sp.wait_ge(s_xi, 1)
            sp.dma_start(xi[:, 2:P + 2], x).then_inc(s_x, 16)
            sp.dma_start(xi[1:P, 0:2], x[0:P - 1, P - 2:P]).then_inc(s_x, 16)
            sp.dma_start(xi[0:P - 1, P + 2:P + 3], x[1:P, 0:1], allow_slow_non_contiguous=True).then_inc(s_x, 16)
            sp.dma_start(small_w[:, 0, :], basis_t).then_inc(s_small, 16)
            sp.dma_start(small_w[:, 1:5, :], coeff_t).then_inc(s_small, 16)
            sp.dma_start(proj[:, :, :], proj_t).then_inc(s_small, 16)
            sp.dma_start(wg[:, :], wg_t).then_inc(s_small, 16)
            for n in [1, 0] + list(range(2, len(blocks))):
                if n == 0:
                    sp.wait_ge(s_av, 1)
                if n >= 2:
                    sp.wait_ge(s_split_lo, n - 1)
                sp.dma_start(stage[:, n % 2, 0:blocks[n][2].shape[-1]], blocks[n][2]).then_inc(s_stage[n % 2], 16)
            sp.sem_inc(s_room, 1)
            with sp.Fori(0, SEQS) as i:
                sp.wait_ge(s_res, i + 2)
                sp.sem_inc(steps["sp"], 1)
                sp.dma_start(out[i, :, :, :], result[:, :, :]).then_inc(s_out, 16)
                sp.wait_ge(s_out, i * 16 + 16)
                sp.sem_inc(s_room, 1)
            sp.wait_ge(s_out, 16 * SEQS)

        @block.gpsimd
        def _(pool):
            def wait_step(semaphore, value):
                pool.wait_ge(semaphore, value)
                pool.sem_inc(steps["pool"], 1)

            pool.memset(xi[:, :], 0).then_inc(s_xi, 1)
            pool.memset(ones_row[:, :], 1.0).then_inc(s_ident, 1)
            pool.memset(ident[:, :], 0.0).then_inc(s_const, 1)
            pool.wait_ge(s_const, 1)
            pool.affine_select(out=ident[:, :], in_=ident[:, :], compare_op=ALU.not_equal, fill=1.0,
                               base=0, pattern=[[-1, P]], channel_multiplier=1).then_inc(s_ident, 1)
            pool.memset(ids[:, :, SEQS * CHUNKS:], 0).then_inc(s_const, 1)
            pool.memset(minus_half[:, :], -0.5).then_inc(s_const, 1)
            pool.memset(dcol[:, 0:1], E_NUMBER).then_inc(s_const, 1)
            pool.iota(dcol[:, 3:4], [[0, 1]], base=0, channel_multiplier=1,
                      allow_small_or_imprecise_dtypes=True).then_inc(s_const, 1)
            pool.memset(decay_chunk[:, :], float(P)).then_inc(s_const, 1)
            pool.iota(power[:, 0, :], [[-1, P]], base=-1, channel_multiplier=1,
                      allow_small_or_imprecise_dtypes=True).then_inc(s_const, 1)
            pool.iota(power[:, 1, :], [[-1, P]], base=P - 1, channel_multiplier=0,
                      allow_small_or_imprecise_dtypes=True).then_inc(s_const, 1)
            pool.memset(decay_mask[:, :], 1.0).then_inc(s_const, 1)
            pool.wait_ge(s_const, 9)
            pool.tensor_scalar(power[:, 0, :], power[:, 0, :], 0.0, None, ALU.max).then_inc(s_const, 1)

            pool.wait_ge(s_spread, 1)
            pool.tensor_tensor(dcol[:, 2:3], dcol[:, 0:1], dcol[:, 1:2], ALU.pow).then_inc(s_pow, 1)

            def take_index(s):
                pool.tensor_copy(idx[:, :].rearrange("p (n c) -> p n c", n=NGRAMS),
                                 ids[:, :, bass.ds(s * CHUNKS, CHUNKS)]).then_inc(s_idx, 1)

            def gather(g):
                n, c = divmod(g, CHUNKS)
                pool.indirect_dma_start(gath[:, n, c, :], None, emb[n],
                                        bass.IndirectOffsetOnAxis(ap=idx[:, g:g + 1], axis=0)).then_inc(s_gath, 16)

            def norm_scale(done, value):
                wait_step(s_mom, value)
                pool.tensor_scalar(var_eps[:, :], moments[:, :, 1], EPS, None, ALU.add).then_inc(s_var, 1)
                pool.wait_ge(s_var, value)
                pool.tensor_tensor(rstd[:, :], var_eps[:, :], minus_half[:, :], ALU.pow).then_inc(s_rstd, 1)

            def decayed_input(value):
                wait_step(s_xn, value)
                pool.tensor_scalar(xn_in[:, :, :], xn[:, 1:CHUNKS, :], decay_in[:, 0:1], None,
                                   ALU.mult).then_inc(s_xn_in, 1)

            def x_low(par, k):
                wait_step(s_x_hi, k)
                pool.tensor_tensor(x_lo[:, par, :], xn_t[:, :], x_hi[:, par, :].bitcast(F32),
                                   ALU.subtract).then_inc(s_x_lo, 1)

            def hidden_low(q, u):
                pool.wait_ge(s_hid_hi, u + 1)
                pool.tensor_tensor(hid_lo[:, hbuf_of(q), :], hid[:, q % 2, :],
                                   hid_hi[:, hbuf_of(q), :].bitcast(F32), ALU.subtract).then_inc(s_hid_lo, 1)

            PART = 16
            pool.memset(zeros, 0.0).then_inc(s_const, 1)
            pool.wait_ge(s_const, 11)
            for n in range(EXPERTS // PART):
                pool.affine_select(out=half_pick, in_=zeros, compare_op=ALU.not_equal, fill=1.0, base=-PART * n,
                                   pattern=[[-1, PART], [0, INTER]], channel_multiplier=1).then_inc(s_const, 1)
                pool.wait_ge(s_const, 12 + 2 * n)
                pool.affine_select(out=pick[:, n * PART * INTER:(n + 1) * PART * INTER].rearrange("p (j m) -> p j m", m=INTER),
                                   in_=half_pick, compare_op=ALU.not_equal, fill=1.0, base=-EXPERTS - PART * n,
                                   pattern=[[-1, PART], [0, INTER]], channel_multiplier=1).then_inc(s_const, 1)
                pool.wait_ge(s_const, 13 + 2 * n)
            pool.memset(emb_t[:, :, :], 0.0).then_inc(s_ident, 1)

            pool.wait_ge(s_ids, 1)
            take_index(0)
            pool.wait_ge(s_idx, 1)
            for g in range(GATHERS):
                gather(g)

            pool.wait_ge(s_decay, 1)
            pool.tensor_scalar(decay_out[:, :], decay_mask[:, :], decay[:, 0:1], None, ALU.mult).then_inc(s_const, 1)
            pool.tensor_tensor(decay_in[:, :], decay[:, :], dcol[:, 3:4], ALU.pow).then_inc(s_pow, 1)
            pool.tensor_tensor(decay_chunk[:, :], decay[:, :], decay_chunk[:, :], ALU.pow).then_inc(s_pow, 1)
            pool.wait_ge(s_const, 20)
            pool.tensor_tensor(decay_mask[:, :], decay_out[:, :], power[:, 0, :], ALU.pow).then_inc(s_pow, 1)
            pool.wait_ge(s_pow, 4)
            pool.tensor_tensor(decay_out[:, :], decay_out[:, :], power[:, 1, :], ALU.pow).then_inc(s_pow, 1)
            pool.affine_select(out=decay_mask[:, :], in_=decay_mask[:, :], compare_op=ALU.is_gt, fill=0.0,
                               base=0, pattern=[[-1, P]], channel_multiplier=1).then_inc(s_pow, 1)

            pool.wait_ge(s_gath, 16 * GATHERS)
            take_index(1)
            pool.wait_ge(s_idx, 2)
            pool.wait_ge(s_emb_ps, NGRAMS)
            for g in range(GATHERS):
                gather(g)
            norm_scale(s_rstd, 1)
            decayed_input(1)
            norm_scale(s_rstd, 2)
            x_low(0, 1)
            for q in range(LEAD - 1):
                hidden_low(q, q)

            with pool.Fori(0, SEQS) as i:
                nxt = pool.snap((i + 1) % 2)
                tile0 = pool.snap(i * TILES)
                for p in range(TILES):
                    if p == INDEX:
                        wait_step(s_gath, i * (16 * GATHERS) + 2 * 16 * GATHERS)
                        take_index(i + 2)
                    if p == EMBED_P + 1:
                        norm_scale(s_rstd, i * 2 + 3)
                    if p == GATHER:
                        wait_step(s_idx, i + 3)
                        wait_step(s_emb_ps, i * NGRAMS + 2 * NGRAMS)
                    if GATHER <= p < GATHER + GATHERS:
                        gather(p - GATHER)
                    if p == XNT_1:
                        decayed_input(i * 2 + 3)
                    if p == PROJECT + 1:
                        norm_scale(s_rstd, i * 2 + 4)
                    if p == XNT_2 + 2:
                        x_low(nxt, i + 2)
                    hidden_low(tile_of(p - 1)[1], tile0 + (p + LEAD - 1))
            pool.wait_ge(s_gath, 16 * GATHERS * (SEQS + 2))

        @block.scalar
        def _(act):
            def wait_step(semaphore, value):
                act.wait_ge(semaphore, value)
                act.sem_inc(steps["act"], 1)

            def emb_out(n, value):
                first, end = VALID[n]
                act.wait_ge(s_emb_ps, value)
                act.activation(emb_t[:, n, first:end], ps_a[:, first:end], ACT.Copy).then_inc(s_emb_act, 1)

            def copy_out(dst, src, ready, k, done):
                act.wait_ge(ready, k)
                act.activation(dst, src, ACT.Copy).then_inc(done, 1)

            def x_high(par, k):
                wait_step(s_xnt2, k)
                act.activation(x_hi[:, par, :], xn_t[:, :], ACT.Copy).then_inc(s_x_hi, 1)

            def exponents(k):
                act.wait_ge(s_shift, k)
                act.activation(expo[:, :, :], expo[:, :, :], ACT.Exp).then_inc(s_exp, 1)

            def comb_out(par, k):
                wait_step(s_combt_ps, k)
                act.activation(comb_t[:, par, :], ps_a[:, :], ACT.Copy).then_inc(s_combt, 1)

            def gate_silu(q, u):
                act.wait_ge(s_gate_ps, u + 1)
                if not isinstance(u, int) or u >= 2:
                    act.wait_ge(s_product, u - 1)
                act.activation(gate[:, q % 2, :], ps_gate[:, q % 2, :], ACT.Silu).then_inc(s_gate, 1)

            def hidden_high(q, u, hid_count):
                if q < ROUTED:
                    act.wait_ge(s_hid, hid_count)
                else:
                    act.wait_ge(s_product, u + 1)
                act.wait_ge(s_down, u + 1)
                act.activation(hid_hi[:, hbuf_of(q), :], hid[:, q % 2, :], ACT.Copy).then_inc(s_hid_hi, 1)

            act.sem_inc(s_y_free, 1)
            for n, (high, _, _) in enumerate(blocks):
                act.wait_ge(s_stage[n % 2], 16 * (n // 2 + 1))
                act.activation(high, stage[:, n % 2, 0:high.shape[-1]], ACT.Copy).then_inc(s_split_hi, 1)
            act.wait_ge(s_ident, 3)
            emb_out(0, 1)
            emb_out(2, 3)
            copy_out(xn_t[:, :], ps_a[:, :], s_xnt1_ps, 1, s_xnt1)
            copy_out(keyed_t[:, :], ps_b[:, :], s_key_ps, 1, s_key)
            copy_out(keyed_t[:, :], ps_a[:, :], s_got_ps, 1, s_got)
            copy_out(xn_t[:, :], ps_a[:, :], s_xnt2_ps, 1, s_xnt2)
            x_high(0, 1)
            exponents(1)
            comb_out(0, 1)
            for q in range(LEAD):
                gate_silu(q, q)
                if q < LEAD - 1:
                    hidden_high(q, q, q + 1)

            with act.Fori(0, SEQS) as i:
                nxt = act.snap((i + 1) % 2)
                tile0 = act.snap(i * TILES)
                routed0 = act.snap(i * ROUTED)
                for p in range(TILES):
                    if p == TILES - 1:
                        act.wait_ge(s_down, tile0 + (TILES + LEAD))
                        act.activation(y_t[:, :], ps_y[:, :], ACT.Copy).then_inc(s_y_free, 1)
                    gate_silu(tile_of(p)[1], tile0 + (p + LEAD))
                    later, q = tile_of(p - 1)
                    hidden_high(q, tile0 + (p + LEAD - 1), routed0 + (later * ROUTED + q + 1))
                    if p == EMBED_T[0]:
                        emb_out(0, i * NGRAMS + (NGRAMS + 1))
                    if p == EMBED_T[2]:
                        emb_out(2, i * NGRAMS + 2 * NGRAMS)
                    if p == XNT_1:
                        copy_out(xn_t[:, :], ps_a[:, :], s_xnt1_ps, i + 2, s_xnt1)
                    if p == KEYED:
                        copy_out(keyed_t[:, :], ps_b[:, :], s_key_ps, i + 2, s_key)
                    if p == RETRIEVE:
                        copy_out(keyed_t[:, :], ps_a[:, :], s_got_ps, i + 2, s_got)
                    if p == XNT_2:
                        copy_out(xn_t[:, :], ps_a[:, :], s_xnt2_ps, i + 2, s_xnt2)
                    if p == XNT_2 + 1:
                        x_high(nxt, i + 2)
                    if p == ROUTE + 1:
                        exponents(i + 2)
                    if p == COMB_T:
                        comb_out(nxt, i + 2)

        @block.vector
        def _(dve):
            def modulo(dst, v, quotient, f):
                dve.drain()
                dve.tensor_scalar(quotient, v, 1.0 / VOCAB, None, ALU.mult)
                dve.drain()
                dve.scalar_tensor_tensor(out=dst, in0=quotient, scalar=-float(VOCAB), in1=v,
                                         op0=ALU.mult, op1=ALU.add)
                dve.drain()
                dve.tensor_scalar(f, dst, 0.0, float(VOCAB), ALU.is_lt, ALU.mult)
                dve.drain()
                dve.tensor_tensor(dst, dst, f, ALU.add)
                dve.drain()
                dve.tensor_scalar(f, dst, float(VOCAB), -float(VOCAB), ALU.is_ge, ALU.mult)
                dve.drain()
                dve.tensor_tensor(dst, dst, f, ALU.add)
                dve.drain()

            def roll(dst, hashed, token):
                n = dst.shape[-1]
                v = tmp_f[:, 1, 0:n]
                dve.scalar_tensor_tensor(out=v, in0=hashed, scalar=BASE, in1=token, op0=ALU.mult, op1=ALU.add)
                modulo(dst, v, tmp_i[:, 0:n], tmp_f[:, 0, 0:n])

            dve.wait_ge(s_x, 48)
            dve.tensor_copy(xf[:, 0, :], xi[:, :])
            modulo(xf[:, 1, :], xf[:, 0, :], tmp_i[:, :], tmp_f[:, 0, :])
            roll(xf[:, 2, 1:W], xf[:, 1, 0:W - 1], xf[:, 0, 1:W])
            roll(xf[:, 3, 1:W - 1], xf[:, 2, 1:W - 1], xf[:, 0, 2:W])
            roll(tmp_f[:, 2, 2:W - 1], xf[:, 3, 1:W - 2], xf[:, 0, 3:W])
            dve.tensor_copy(id_f[:, 0, :], xf[:, 2, 2:P + 2])
            dve.tensor_copy(id_f[:, 1, :], xf[:, 3, 2:P + 2])
            dve.tensor_copy(id_f[:, 2, :], tmp_f[:, 2, 2:P + 2]).then_inc(s_hash, 1)
            dve.wait_ge(s_hash_ps, 1)
            dve.tensor_copy(ids[:, :, 0:P], ps_a[:, 0:NGRAMS * P].rearrange("p (n t) -> p n t", n=NGRAMS)).then_inc(s_ids, 1)

            dve.wait_ge(s_spread_ps, 1)
            dve.tensor_copy(bias[:, :], ps_b[:, 0:P])
            dve.tensor_copy(scale[:, :], ps_b[:, P + 1:P + 2])
            dve.tensor_scalar(dcol[:, 1:2], ps_b[:, P:P + 1], -1.0, None, ALU.mult).then_inc(s_spread, 1)
            dve.wait_ge(s_pow, 1)
            dve.tensor_scalar(decay[:, :], dcol[:, 2:3], 1.0, None, ALU.add)
            dve.drain()
            dve.reciprocal(decay[:, :], decay[:, :]).then_inc(s_decay, 1)

            dve.wait_ge(s_wt_ps, 1)
            dve.tensor_copy(w_t, ps_gate[:, 0, :].rearrange("p (a b) -> p a b", a=4)).then_inc(s_wt, 1)
            dve.wait_ge(s_av_ps, 1)
            dve.tensor_copy(qk_w[:, :], ps_gate[:, 1, 0:P])
            dve.tensor_scalar(vo_w[:, :], ps_gate[:, 1, P:2 * P], scale[:, 0:1], None, ALU.mult).then_inc(s_av, 1)

            for n, (high, low, _) in enumerate(blocks):
                dve.wait_ge(s_split_hi, n + 1)
                dve.tensor_tensor(low, stage[:, n % 2, 0:low.shape[-1]], high.bitcast(F32), ALU.subtract).then_inc(s_split_lo, 1)

            def emb_out(value):
                first, end = VALID[1]
                dve.wait_ge(s_emb_ps, value)
                dve.tensor_copy(emb_t[:, 1, first:end], ps_b[:, first:end]).then_inc(s_emb_dve, 1)

            def moments_of(t):
                dve.drain()
                for c in range(CHUNKS):
                    dve.bn_stats(out=stats[:, c, :], in_=t[:, c, :])
                dve.drain()
                for c in range(CHUNKS):
                    last = dve.bn_aggr(out=moments[:, c, :], in_=stats[:, c, :])
                last.then_inc(s_mom, 1)

            def embedded(k):
                dve.wait_ge(s_h1_ps, k)
                dve.tensor_tensor(h1[:, :, :], chunked(ps_b), bias[:, None, :].to_broadcast([P, CHUNKS, P]), ALU.add)
                moments_of(h1)

            def normalise(t, value):
                dve.wait_ge(s_rstd, value)
                for c in range(CHUNKS):
                    last = dve.tensor_scalar(xn[:, c, :], t[:, c, :], moments[:, c, 0:1], rstd[:, c:c + 1],
                                             ALU.subtract, ALU.mult)
                last.then_inc(s_xn, 1)

            def key_decayed(k):
                dve.wait_ge(s_key, k)
                dve.tensor_tensor(keyed_out[:, :, :], chunked(keyed_t)[:, 0:CHUNKS - 1, :],
                                  decay_out[:, None, :].to_broadcast([P, CHUNKS - 1, P]),
                                  ALU.mult).then_inc(s_key_out, 1)

            def mask_scores(k):
                dve.wait_ge(s_score_ps, k)
                dve.tensor_tensor(scores[:, :, :], chunked(ps_a), decay_mask[:, None, :].to_broadcast([P, CHUNKS, P]),
                                  ALU.mult).then_inc(s_score, 1)

            def chain_states(k):
                dve.wait_ge(s_state_ps, k)
                last = dve.tensor_copy(state[:, CHUNKS - 2, :], ps_b[:, (CHUNKS - 2) * P:(CHUNKS - 1) * P])
                for j in range(CHUNKS - 3, -1, -1):
                    dve.drain()
                    last = dve.scalar_tensor_tensor(out=state[:, j, :], in0=state[:, j + 1, :],
                                                    scalar=decay_chunk[:, 0:1], in1=ps_b[:, j * P:(j + 1) * P],
                                                    op0=ALU.mult, op1=ALU.add)
                last.then_inc(s_state, 1)

            def half(t, par):
                return t[:, par, :].rearrange("p (c n) -> p c n", c=CHUNKS)

            def attended(par, k):
                dve.wait_ge(s_h2_ps, k)
                dve.tensor_tensor(half(h2, par), chunked(ps_b), h1[:, :, :], ALU.add)
                moments_of(half(h2, par))

            def find_top(k):
                dve.wait_ge(s_route_ps, k)
                dve.tensor_copy(logits[:, :, :], ps_b[:, 0:CHUNKS * EXPERTS].rearrange("p (c e) -> p c e", c=CHUNKS))\
                   .then_inc(s_logits, 1)
                dve.drain()
                for c in range(CHUNKS):
                    dve.max(top[:, c, :], logits[:, c, :])

            def strike_top():
                dve.drain()
                dve.tensor_tensor(expo[:, :, :], logits[:, :, :],
                                  top[:, :, 0:1].to_broadcast([P, CHUNKS, EXPERTS]), ALU.subtract).then_inc(s_shift, 1)
                dve.memset(top[:, :, TOP_K:8], -HUGE)
                dve.drain()
                for c in range(CHUNKS):
                    dve.match_replace(out=struck[:, c, :], in_to_replace=top[:, c, :], in_values=logits[:, c, :],
                                      imm_value=-HUGE)
                dve.drain()
                dve.tensor_tensor(struck[:, :, :], struck[:, :, :], logits[:, :, :], ALU.not_equal)

            def chosen_sum(k):
                dve.drain()
                dve.wait_ge(s_exp, k)
                dve.tensor_tensor(struck[:, :, :], struck[:, :, :], expo[:, :, :], ALU.mult)
                dve.drain()
                dve.tensor_reduce(total[:, :], struck[:, :, :], AX_X, ALU.add)
                dve.drain()
                dve.reciprocal(inv_total[:, :], total[:, :])

            def weigh():
                dve.drain()
                dve.tensor_tensor(struck[:, :, :], struck[:, :, :],
                                  inv_total[:, :, None].to_broadcast([P, CHUNKS, EXPERTS]), ALU.mult)
                dve.drain()
                dve.tensor_copy(comb[:, :, 0, :], struck[:, :, :])
                dve.drain()
                dve.tensor_tensor(comb[:, :, 1, :], struck[:, :, :], comb[:, :, 0, :].bitcast(F32),
                                  ALU.subtract).then_inc(s_comb, 1)

            def hidden(q, u, hid_count):
                if not isinstance(u, int) or u >= 2:
                    dve.wait_ge(s_hid_lo, u - 1)
                dve.wait_ge(s_gate, u + 1)
                dve.wait_ge(s_lin_ps, u + 1)
                dst = product if q < ROUTED else hid
                dve.tensor_tensor(dst[:, q % 2, :], gate[:, q % 2, :], ps_lin[:, q % 2, :], ALU.mult).then_inc(s_product, 1)
                if q < ROUTED:
                    dve.drain()
                    dve.wait_ge(s_comb_ps, hid_count)
                    dve.tensor_tensor(hid[:, q % 2, :], product[:, q % 2, :], ps_comb[:, :], ALU.mult).then_inc(s_hid, 1)

            emb_out(2)
            embedded(1)
            normalise(h1, 1)
            dve.wait_ge(s_pow, 6)
            key_decayed(1)
            mask_scores(1)
            chain_states(1)
            attended(0, 1)
            normalise(half(h2, 0), 2)
            find_top(1)
            strike_top()
            chosen_sum(1)
            weigh()
            for q in range(LEAD):
                hidden(q, q, q + 1)
            dve.sem_inc(s_res, 1)

            with dve.Fori(0, SEQS) as i:
                cur = dve.snap(i % 2)
                nxt = dve.snap((i + 1) % 2)
                tile0 = dve.snap(i * TILES)
                routed0 = dve.snap(i * ROUTED)
                for p in range(TILES):
                    later, q = tile_of(p)
                    hidden(q, tile0 + (p + LEAD), routed0 + (later * ROUTED + q + 1))
                    if p == EMBED_T[1]:
                        emb_out(i * NGRAMS + (NGRAMS + 2))
                    if p == EMBED_P:
                        embedded(i + 2)
                    if p == EMBED_P + 2:
                        normalise(h1, i * 2 + 3)
                    if p == KEYED:
                        key_decayed(i + 2)
                    if p == SCORE:
                        mask_scores(i + 2)
                    if p == STATE:
                        chain_states(i + 2)
                    if p == PROJECT:
                        attended(nxt, i + 2)
                    if p == PROJECT + 2:
                        normalise(half(h2, nxt), i * 2 + 4)
                    if p == ROUTE:
                        find_top(i + 2)
                    if p == ROUTE + 1:
                        strike_top()
                    if p == ROUTE + 3:
                        chosen_sum(i + 2)
                    if p == ROUTE + 4:
                        weigh()
                dve.wait_ge(s_res_ps, i + 1)
                dve.wait_ge(s_room, i + 1)
                dve.tensor_tensor(result[:, :, :], chunked(ps_b), half(h2, cur), ALU.add).then_inc(s_res, 1)

        @block.tensor
        def _(pe):
            def chunk(t, c):
                return t[:, c * P:(c + 1) * P]

            def transposes(dst, parts, signal):
                for c, part in enumerate(parts):
                    last = pe.transpose(chunk(dst, c), part, ident[:, :])
                last.then_inc(signal, 1)

            pe.wait_ge(s_ident, 2)
            pe.wait_ge(s_hash, 1)
            transposes(ps_a, [id_f[:, n, :] for n in range(NGRAMS)], s_hash_ps)
            pe.wait_ge(s_row, 16)
            pe.matmul(ps_b[:, 0:P + 2], ones_row[:, :], row[:, :], start=True, stop=True).then_inc(s_spread_ps, 1)
            pe.wait_ge(s_small, 64)
            for m in range(4):
                last = pe.matmul(ps_gate[:, 0, m * P:(m + 1) * P], small_w[:, 1 + m, :], small_w[:, 0, :],
                                 start=True, stop=True)
            last.then_inc(s_wt_ps, 1)
            pe.wait_ge(s_wt, 1)
            for m in range(2):
                last = pe.matmul(ps_gate[:, 1, m * P:(m + 1) * P], w_t[:, 2 * m, :], w_t[:, 2 * m + 1, :],
                                 start=True, stop=True)
            last.then_inc(s_av_ps, 1)

            def embed_t(n):
                transposes((ps_a, ps_b)[n % 2], [gath[:, n, c, :] for c in range(CHUNKS)], s_emb_ps)

            def embed_project():
                for c in range(CHUNKS):
                    for n in range(NGRAMS):
                        last = pe.matmul(chunk(ps_b, c), emb_t[:, n, c * P:(c + 1) * P], proj[:, n, :],
                                         start=(n == 0), stop=(n == NGRAMS - 1))
                last.then_inc(s_h1_ps, 1)

            def xn_transpose(value, signal):
                pe.wait_ge(s_xn, value)
                transposes(ps_a, [xn[:, c, :] for c in range(CHUNKS)], signal)

            def keyed(k):
                pe.wait_ge(s_xnt1, k)
                pe.matmul(ps_b[:, :], qk_w[:, :], xn_t[:, :], start=True, stop=True).then_inc(s_key_ps, 1)

            def score(k):
                pe.wait_ge(s_key, k)
                for c in range(CHUNKS):
                    last = pe.matmul(chunk(ps_a, c), chunk(xn_t, c), chunk(keyed_t, c), start=True, stop=True)
                last.then_inc(s_score_ps, 1)

            def chunk_sums(k):
                pe.wait_ge(s_xn_in, k)
                for j in range(CHUNKS - 1):
                    last = pe.matmul(chunk(ps_b, j), xn_in[:, j, :], xn[:, j + 1, :], start=True, stop=True)
                last.then_inc(s_state_ps, 1)

            def retrieve(k):
                pe.wait_ge(s_score, k)
                pe.wait_ge(s_state, k)
                pe.wait_ge(s_key_out, k)
                for c in range(CHUNKS):
                    last = pe.matmul(chunk(ps_a, c), xn[:, c, :], scores[:, c, :], start=True, stop=(c == CHUNKS - 1))
                    if c < CHUNKS - 1:
                        last = pe.matmul(chunk(ps_a, c), state[:, c, :], keyed_out[:, c, :], start=False, stop=True)
                last.then_inc(s_got_ps, 1)

            def project(k):
                pe.wait_ge(s_got, k)
                for c in range(CHUNKS):
                    last = pe.matmul(chunk(ps_b, c), chunk(keyed_t, c), vo_w[:, :], start=True, stop=True)
                last.then_inc(s_h2_ps, 1)

            def route(k):
                pe.wait_ge(s_xnt2, k)
                for c in range(CHUNKS):
                    last = pe.matmul(ps_b[:, c * EXPERTS:(c + 1) * EXPERTS], chunk(xn_t, c), wg[:, :],
                                     start=True, stop=True)
                last.then_inc(s_route_ps, 1)

            def comb_transpose(k):
                pe.wait_ge(s_comb, k)
                transposes(ps_a, [comb[:, c, :, :].rearrange("p a e -> p (a e)").bitcast(F32) for c in range(CHUNKS)],
                           s_combt_ps)

            def up(q, par, u, routed):
                cols = slice(q * P, (q + 1) * P)
                for m, (ps, used, signal) in enumerate(((ps_gate, s_gate, s_gate_ps), (ps_lin, s_product, s_lin_ps))):
                    if not isinstance(u, int) or u >= 2:
                        pe.wait_ge(used, u - 1)
                    dst = ps[:, q % 2, :]
                    pe.matmul(dst, up_hi[:, m, cols], x_hi[:, par, :], start=True, stop=False)
                    pe.matmul(dst, up_hi[:, m, cols], x_lo[:, par, :], start=False, stop=False)
                    pe.matmul(dst, up_lo[:, m, cols], x_hi[:, par, :], start=False, stop=True).then_inc(signal, 1)
                if q < ROUTED:
                    if not isinstance(u, int) or u >= 1:
                        pe.wait_ge(s_hid, routed)
                    pe.matmul(ps_comb[:, :], pick[:, cols], comb_t[:, par, :], start=True, stop=True).then_inc(s_comb_ps, 1)

            def down_tile(q, u):
                cols = slice(q * P, (q + 1) * P)
                pe.wait_ge(s_hid_lo, u + 1)
                pe.matmul(ps_y[:, :], down_hi[:, cols], hid_hi[:, hbuf_of(q), :], start=(q == 0), stop=False)
                pe.matmul(ps_y[:, :], down_hi[:, cols], hid_lo[:, hbuf_of(q), :], start=False, stop=False)
                pe.matmul(ps_y[:, :], down_lo[:, cols], hid_hi[:, hbuf_of(q), :], start=False,
                          stop=(q == TILES - 1)).then_inc(s_down, 1)

            pe.wait_ge(s_gath, 16 * GATHERS)
            embed_t(0)
            pe.wait_ge(s_spread, 1)
            embed_t(1)
            pe.wait_ge(s_emb_act, 1)
            embed_t(2)
            pe.wait_ge(s_emb_act, 2)
            pe.wait_ge(s_emb_dve, 1)
            embed_project()
            xn_transpose(1, s_xnt1_ps)
            pe.wait_ge(s_av, 1)
            keyed(1)
            score(1)
            chunk_sums(1)
            retrieve(1)
            project(1)
            xn_transpose(2, s_xnt2_ps)
            route(1)
            comb_transpose(1)
            pe.wait_ge(s_split_lo, len(blocks))
            pe.wait_ge(s_x_lo, 1)
            pe.wait_ge(s_combt, 1)
            pe.sem_inc(s_down, LEAD)
            for q in range(LEAD):
                up(q, 0, q, q)

            with pe.Fori(0, SEQS) as i:
                cur = pe.snap(i % 2)
                nxt = pe.snap((i + 1) % 2)
                tile0 = pe.snap(i * TILES)
                routed0 = pe.snap(i * ROUTED)
                for p in range(TILES):
                    if p == EMBED_T[0]:
                        pe.wait_ge(s_gath, i * (16 * GATHERS) + 2 * 16 * GATHERS)
                        pe.wait_ge(s_combt, i + 1)
                        embed_t(0)
                    if p == EMBED_T[1]:
                        pe.wait_ge(s_res, i + 1)
                        embed_t(1)
                    if p == EMBED_T[2]:
                        pe.wait_ge(s_emb_act, i * 2 + 3)
                        embed_t(2)
                    if p == EMBED_P:
                        pe.wait_ge(s_emb_act, i * 2 + 4)
                        pe.wait_ge(s_emb_dve, i + 2)
                        embed_project()
                    if p == XNT_1:
                        xn_transpose(i * 2 + 3, s_xnt1_ps)
                    if p == KEYED:
                        keyed(i + 2)
                    if p == SCORE:
                        score(i + 2)
                    if p == STATE:
                        chunk_sums(i + 2)
                    if p == RETRIEVE:
                        retrieve(i + 2)
                    if p == PROJECT:
                        project(i + 2)
                    if p == XNT_2:
                        xn_transpose(i * 2 + 4, s_xnt2_ps)
                    if p == ROUTE:
                        route(i + 2)
                    if p == COMB_T:
                        comb_transpose(i + 2)
                    if p == 0:
                        pe.wait_ge(s_y_free, i + 1)
                    later, q = tile_of(p)
                    if p == TILES - 1:
                        down_tile(p, tile0 + p)
                    if later and q == 0:
                        pe.wait_ge(s_x_lo, i + 2)
                        pe.wait_ge(s_combt, i + 2)
                    up(q, nxt if later else cur, tile0 + (p + LEAD), routed0 + (later * ROUTED + q))
                    if p < TILES - 1:
                        down_tile(p, tile0 + p)
                pe.wait_ge(s_y_free, i + 2)
                pe.wait_ge(s_logits, i + 2)
                transposes(ps_b, [chunk(y_t, c) for c in range(CHUNKS)], s_res_ps)


def kernel(**inputs):
    import concourse.bacc as bacc
    from concourse.bass_utils import run_bass_kernel_spmd

    nc = bacc.Bacc("TRN2", target_bir_lowering=False, num_devices=1)
    a = {k: np.asarray(v) for k, v in inputs.items()}

    def hidden_major(name, shared):
        w = a[name].reshape(EXPERTS * INTER, P)
        return np.concatenate([w, a[shared]], axis=0).T

    down = np.concatenate([a["L0_ffn_w2"].reshape(EXPERTS * INTER, P), a["L0_ffn_w_sd"].T], axis=0)
    arrays = {
        "x": a["x"].reshape(P, P),
        "emb_2": a["L0_tok_emb_2"], "emb_3": a["L0_tok_emb_3"], "emb_4": a["L0_tok_emb_4"],
        "proj_t": a["L0_tok_proj_w"].T.reshape(NGRAMS, P, P).transpose(1, 0, 2),
        "rows": np.concatenate([a["L0_tok_proj_b"].reshape(1, P), a["L0_attn_decay_logit"].reshape(1, 1),
                                a["L0_attn_out_scale"].reshape(1, 1)], axis=1),
        "basis_t": a["L0_attn_basis"].T,
        "coeff_t": np.stack([a[f"L0_attn_{m}_coeffs"].T for m in "qkvo"], axis=1),
        "wg_t": a["L0_ffn_w_gate"].T,
        "up_gate": hidden_major("L0_ffn_w1", "L0_ffn_w_sg"),
        "up_lin": hidden_major("L0_ffn_w3", "L0_ffn_w_su"),
        "down": down.reshape(TILES, P, P).transpose(1, 0, 2).reshape(P, TILES * P),
    }
    arrays = {k: np.ascontiguousarray(v) for k, v in arrays.items()}
    ap = {k: nc.dram_tensor(k, v.shape, mybir.dt.from_np(v.dtype), kind="ExternalInput").ap()
          for k, v in arrays.items()}
    out = nc.dram_tensor("out", (SEQS, SEQ_LEN, P), F32, kind="ExternalOutput").ap()
    build(nc, ap["x"], [ap["emb_2"], ap["emb_3"], ap["emb_4"]], ap["proj_t"], ap["rows"], ap["basis_t"],
          ap["coeff_t"], ap["wg_t"], ap["up_gate"], ap["up_lin"], ap["down"],
          out.rearrange("s (c p) d -> s p c d", c=CHUNKS))
    return run_bass_kernel_spmd(nc, [arrays], core_ids=[0]).results[0]["out"]
```

```python
from contextlib import ExitStack

import concourse.bass as bass
import numpy as np
from concourse import mybir

ALU = mybir.AluOpType
ACT = mybir.ActivationFunctionType
AX_X = mybir.AxisListType.X
F32 = mybir.dt.float32
F32R = mybir.dt.float32r
I32 = mybir.dt.int32
U32 = mybir.dt.uint32

P = 128
SEQS, SEQ_LEN = 32, 512
CHUNKS = SEQ_LEN // P
VOCAB, BASE = 25000, 64.0
NGRAMS = 3
EXPERTS, INTER, TOP_K = 64, 64, 6
ROUTED = EXPERTS * INTER // P
SHARED = 256 // P
TILES = ROUTED + SHARED
BLOCK = 12
LEAD = 3
POWERS = 2 * P + 1
EPS = 1e-5
HUGE = 3e38
E_NUMBER = float(np.e)

VALID = [(1, SEQ_LEN), (1, SEQ_LEN - 1), (2, SEQ_LEN - 1)]

EMBED_T = (0, 0, 1)
EMBED_P = 2
XNT_1 = 8
KEYED = 9
SCORE = 10
STATE = 11
RETRIEVE = 13
PROJECT = 14
XNT_2 = 20
ROUTE = 21
COMB_T = 28
INDEX = 3
GATHER = (4, 6, 8, 10, 12, 14, 18, 20, 22, 24, 26, 28)
AHEAD = 2
COMB_BUFS = 4


def hbuf_of(q):
    return 3 if q == TILES - 1 else q % 3


def build(nc, x, emb, proj_t, rows, basis_t, coeff_t, wg_t, up_gate, up_lin, down, comb_dram, out):
    ctx = ExitStack()
    with ctx:
        def sb(name, shape, dt=F32):
            return ctx.enter_context(nc.sbuf_tensor(name, shape, dt))

        def pb(name, shape, dt=F32):
            return ctx.enter_context(nc.psum_tensor(name, shape, dt))

        def sem(name):
            return ctx.enter_context(nc.semaphore(name))

        up_hi = sb("up_hi", [P, 2, TILES * P], F32R)
        up_lo = sb("up_lo", [P, 2, TILES * P], F32R)
        down_hi = sb("down_hi", [P, TILES * P], F32R)
        down_lo = sb("down_lo", [P, TILES * P], F32R)
        proj = sb("proj", [P, NGRAMS, P])
        wg = sb("wg", [P, EXPERTS])
        qk_w = sb("qk_w", [P, P])
        vo_w = sb("vo_w", [P, P])
        ident = sb("ident", [P, P])
        bias = sb("bias", [P, P])
        powers = sb("powers", [P, POWERS])
        decay_mask = powers[:, 0:P]
        decay_out = powers[:, P:2 * P]
        decay_in = powers[:, 2 * P:2 * P + 1]
        decay_chunk = sb("decay_chunk", [P, 1])
        decay = sb("decay", [P, 1])
        scale = sb("scale", [P, 1])
        minus_half = sb("minus_half", [P, CHUNKS])
        ids = sb("ids", [P, NGRAMS, (SEQS + 2) * CHUNKS], U32)

        row = sb("row", [1, P + 2])
        ones_row = sb("ones_row", [1, P])
        xi = sb("xi", [P, P + 3], I32)
        tmp_i = sb("tmp_i", [P, P + 3], I32)
        dcol = sb("dcol", [P, 3])

        idx = sb("idx", [P, NGRAMS * CHUNKS], U32)
        gath = sb("gath", [P, NGRAMS, CHUNKS, P])
        emb_t = sb("emb_t", [P, NGRAMS, SEQ_LEN])
        h1 = sb("h1", [P, CHUNKS, P])
        stats = sb("stats", [P, CHUNKS, 6])
        moments = sb("moments", [P, CHUNKS, 2])
        var_eps = sb("var_eps", [P, CHUNKS])
        rstd = sb("rstd", [P, CHUNKS])
        xn = sb("xn", [P, CHUNKS, P])
        xn_t = sb("xn_t", [P, SEQ_LEN])
        keyed_t = sb("keyed_t", [P, SEQ_LEN])
        attention = sb("attention", [P, (4 * CHUNKS - 3) * P])
        keyed_out, xn_in, state, scores = (
            attention[:, n * (CHUNKS - 1) * P:end * P].rearrange("p (c n) -> p c n", n=P)
            for n, end in enumerate((CHUNKS - 1, 2 * (CHUNKS - 1), 3 * (CHUNKS - 1), 4 * CHUNKS - 3)))
        logits = sb("logits", [P, CHUNKS, EXPERTS])
        top = sb("top", [P, CHUNKS, 8])
        struck = sb("struck", [P, CHUNKS, EXPERTS])
        expo = sb("expo", [P, CHUNKS, EXPERTS])
        total = sb("total", [P, CHUNKS])
        inv_total = sb("inv_total", [P, CHUNKS])
        comb_t = sb("comb_t", [EXPERTS, SEQ_LEN])

        h2 = sb("h2", [P, 2, SEQ_LEN])
        x_hi = sb("x_hi", [P, 2, SEQ_LEN], F32R)
        x_lo = sb("x_lo", [P, 2, SEQ_LEN], F32R)

        spread = sb("spread", [P, COMB_BUFS, SEQ_LEN])
        work = sb("work", [P, 8 * SEQ_LEN])
        gate = work[:, 0:2 * SEQ_LEN].rearrange("p (a t) -> p a t", a=2)
        product = work[:, 2 * SEQ_LEN:4 * SEQ_LEN].rearrange("p (a t) -> p a t", a=2)
        hid = work[:, 4 * SEQ_LEN:6 * SEQ_LEN].rearrange("p (a t) -> p a t", a=2)
        y_t = work[:, 6 * SEQ_LEN:7 * SEQ_LEN]
        result = work[:, 7 * SEQ_LEN:8 * SEQ_LEN].rearrange("p (c d) -> p c d", c=CHUNKS)
        hid_hi = sb("hid_hi", [P, 4, SEQ_LEN], F32R)
        hid_lo = sb("hid_lo", [P, 4, SEQ_LEN], F32R)

        ps_gate = pb("ps_gate", [P, 2, SEQ_LEN])
        ps_lin = pb("ps_lin", [P, 2, SEQ_LEN])
        ps_y = pb("ps_y", [P, SEQ_LEN])
        ps_a = pb("ps_a", [P, SEQ_LEN])
        ps_b = pb("ps_b", [P, SEQ_LEN])
        ps_c = pb("ps_c", [P, SEQ_LEN])

        def chunked(t):
            return t[:, :].rearrange("p (c n) -> p c n", c=CHUNKS)

        stage = [work[:, 0:BLOCK * P], work[:, BLOCK * P:2 * BLOCK * P]]
        stage.append(attention[:, 0:BLOCK * P])
        spread_flat = spread[:, :, :].rearrange("p a t -> p (a t)")
        small_w = spread_flat[:, 0:5 * P].rearrange("p (a b) -> p a b", a=5)
        w_t = spread_flat[:, 5 * P:9 * P].rearrange("p (a b) -> p a b", a=4)
        exponent = spread_flat[:, 9 * P:9 * P + POWERS].bitcast(I32)
        bit = spread_flat[:, 9 * P + POWERS:9 * P + 2 * POWERS].bitcast(I32)
        no_bit = spread_flat[:, 9 * P + 2 * POWERS:9 * P + 3 * POWERS]
        W = P + 3
        xf = work[:, 2 * BLOCK * P:2 * BLOCK * P + 4 * W].rearrange("p (a t) -> p a t", a=4)
        tmp_f = work[:, 2 * BLOCK * P + 4 * W:2 * BLOCK * P + 7 * W].rearrange("p (a t) -> p a t", a=3)
        id_f = h1[:, 0:NGRAMS, :]

        s_xi = sem("s_xi")
        s_x = sem("s_x")
        s_small = sem("s_small")
        s_row = sem("s_row")
        s_stage = [sem(f"s_stage{b}") for b in range(len(stage))]
        s_split_hi = sem("s_split_hi")
        s_split_lo = sem("s_split_lo")
        s_const = sem("s_const")
        s_ident = sem("s_ident")
        s_pow = sem("s_pow")
        s_spread_ps = sem("s_spread_ps")
        s_spread = sem("s_spread")
        s_power = sem("s_power")
        s_hash = sem("s_hash")
        s_hash_ps = sem("s_hash_ps")
        s_ids = sem("s_ids")
        s_wt_ps = sem("s_wt_ps")
        s_wt = sem("s_wt")
        s_av_ps = sem("s_av_ps")
        s_av = sem("s_av")
        steps = {e: sem("steps_" + e) for e in ("pool", "act", "sp", "pe")}
        s_idx = sem("s_idx")
        s_gath = sem("s_gath")
        s_emb_ps = sem("s_emb_ps")
        s_emb_act = sem("s_emb_act")
        s_emb_dve = sem("s_emb_dve")
        s_h1_ps = sem("s_h1_ps")
        s_mom = sem("s_mom")
        s_var = sem("s_var")
        s_rstd = sem("s_rstd")
        s_xn = sem("s_xn")
        s_xn_in = sem("s_xn_in")
        s_xnt1_ps = sem("s_xnt1_ps")
        s_xnt1 = sem("s_xnt1")
        s_key_ps = sem("s_key_ps")
        s_key = sem("s_key")
        s_key_out = sem("s_key_out")
        s_score_ps = sem("s_score_ps")
        s_score = sem("s_score")
        s_state_ps = sem("s_state_ps")
        s_state = sem("s_state")
        s_got_ps = sem("s_got_ps")
        s_got = sem("s_got")
        s_h2_ps = sem("s_h2_ps")
        s_xnt2_ps = sem("s_xnt2_ps")
        s_xnt2 = sem("s_xnt2")
        s_x_hi = sem("s_x_hi")
        s_x_lo = sem("s_x_lo")
        s_route_ps = sem("s_route_ps")
        s_logits = sem("s_logits")
        s_shift = sem("s_shift")
        s_exp = sem("s_exp")
        s_comb = sem("s_comb")
        s_combt_ps = sem("s_combt_ps")
        s_combt = sem("s_combt")
        s_y_free = sem("s_y_free")
        s_res_ps = sem("s_res_ps")
        s_res = sem("s_res")
        s_stored = sem("s_stored")
        s_spread_w = [sem(f"s_spread_w{b}") for b in range(COMB_BUFS)]
        s_gate_ps = sem("s_gate_ps")
        s_lin_ps = sem("s_lin_ps")
        s_gate = sem("s_gate")
        s_product = sem("s_product")
        s_hid = sem("s_hid")
        s_hid_hi = sem("s_hid_hi")
        s_hid_lo = sem("s_hid_lo")
        s_down = sem("s_down")

        block = ctx.enter_context(nc.Block())

        blocks = []
        for first in range(0, TILES, BLOCK):
            cols = slice(first * P, min(first + BLOCK, TILES) * P)
            for k, src in enumerate((up_gate, up_lin)):
                blocks.append((up_hi[:, k, cols], up_lo[:, k, cols], src[:, cols]))
            blocks.append((down_hi[:, cols], down_lo[:, cols], down[:, cols]))

        stage_of = [n if n < 3 else (n + 1) % 2 for n in range(len(blocks))]
        before = [stage_of[:n].count(b) for n, b in enumerate(stage_of)]

        GATHERS = NGRAMS * CHUNKS
        EARLY = 4

        def tile_of(p):
            return (p + LEAD) // TILES, (p + LEAD) % TILES


        @block.sync
        def _(sp):
            sp.wait_ge(s_xi, 1)
            sp.dma_start(xi[:, 2:P + 2], x).then_inc(s_x, 16)
            sp.dma_start(xi[1:P, 0:2], x[0:P - 1, P - 2:P]).then_inc(s_x, 16)
            sp.dma_start(xi[0:P - 1, P + 2:P + 3], x[1:P, 0:1], allow_slow_non_contiguous=True).then_inc(s_x, 16)
            sp.dma_start(row[:, :], rows).then_inc(s_row, 16)
            sp.dma_start(small_w[:, 0, :], basis_t).then_inc(s_small, 16)
            sp.dma_start(small_w[:, 1:5, :], coeff_t).then_inc(s_small, 16)
            sp.dma_start(proj[:, :, :], proj_t).then_inc(s_small, 16)
            sp.dma_start(wg[:, :], wg_t).then_inc(s_small, 16)
            for n, (_, _, src) in enumerate(blocks):
                b = stage_of[n]
                if before[n]:
                    last = max(m for m in range(n) if stage_of[m] == b)
                    sp.wait_ge(s_split_lo, last + 1)
                sp.dma_start(stage[b][:, 0:src.shape[-1]], src).then_inc(s_stage[b], 16)

            def load_spread(q, par):
                src = comb_dram[par, 2 * q:2 * q + 2, :]
                src = src[None, :, :].to_broadcast([INTER, 2, SEQ_LEN])
                sp.dma_start(spread[:, q % COMB_BUFS, :], src).then_inc(s_spread_w[q % COMB_BUFS], 16)

            sp.wait_ge(s_combt, 1)
            sp.dma_start(comb_dram[0, :, :], comb_t[:, :]).then_inc(s_stored, 16)
            sp.wait_ge(s_stored, 16)
            for q in range(LEAD + AHEAD):
                if q >= COMB_BUFS:
                    sp.wait_ge(s_hid, q - COMB_BUFS + 1)
                load_spread(q, 0)

            with sp.Fori(0, SEQS) as i:
                cur = sp.snap(i % 2)
                nxt = sp.snap((i + 1) % 2)
                routed0 = sp.snap(i * ROUTED)
                for p in range(TILES):
                    later, q = (p + LEAD + AHEAD) // TILES, (p + LEAD + AHEAD) % TILES
                    if p == COMB_T + 1:
                        sp.wait_ge(s_combt, i + 2)
                        sp.sem_inc(steps["sp"], 1)
                        sp.dma_start(comb_dram[nxt, :, :], comb_t[:, :]).then_inc(s_stored, 16)
                    if later and q == 0:
                        sp.wait_ge(s_stored, i * 32 + 32)
                        sp.sem_inc(steps["sp"], 1)
                    if q < ROUTED:
                        sp.wait_ge(s_hid, routed0 + (later * ROUTED + q - COMB_BUFS + 1))
                        sp.sem_inc(steps["sp"], 1)
                        load_spread(q, nxt if later else cur)
                sp.wait_ge(s_res, i + 2)
                sp.sem_inc(steps["sp"], 1)
                sp.dma_start(out[i, :, :, :], result[:, :, :]).then_inc(s_stored, 16)
            sp.wait_ge(s_stored, 16 + 32 * SEQS)
            for b in range(COMB_BUFS):
                sp.wait_ge(s_spread_w[b], 16 * ((SEQS * ROUTED + LEAD + AHEAD - b + COMB_BUFS - 1) // COMB_BUFS))

        @block.gpsimd
        def _(pool):
            def wait_step(semaphore, value):
                pool.wait_ge(semaphore, value)
                pool.sem_inc(steps["pool"], 1)

            pool.memset(xi[:, :], 0).then_inc(s_xi, 1)
            pool.memset(ones_row[:, :], 1.0).then_inc(s_ident, 1)
            pool.memset(ident[:, :], 0.0).then_inc(s_const, 1)
            pool.wait_ge(s_const, 1)
            pool.affine_select(out=ident[:, :], in_=ident[:, :], compare_op=ALU.not_equal, fill=1.0,
                               base=0, pattern=[[-1, P]], channel_multiplier=1).then_inc(s_ident, 1)
            pool.memset(ids[:, :, SEQS * CHUNKS:], 0).then_inc(s_const, 1)
            pool.memset(minus_half[:, :], -0.5).then_inc(s_const, 1)
            pool.memset(dcol[:, 0:1], E_NUMBER).then_inc(s_const, 1)
            pool.iota(exponent[:, 0:P], [[-1, P]], base=-1, channel_multiplier=1).then_inc(s_const, 1)
            pool.iota(exponent[:, P:2 * P], [[-1, P]], base=P - 1, channel_multiplier=0).then_inc(s_const, 1)
            pool.iota(exponent[:, 2 * P:POWERS], [[0, 1]], base=0, channel_multiplier=1).then_inc(s_const, 1)
            pool.memset(emb_t[:, :, :], 0.0).then_inc(s_ident, 1)
            pool.wait_ge(s_const, 4)
            pool.wait_ge(s_spread, 1)
            pool.tensor_tensor(dcol[:, 2:3], dcol[:, 0:1], dcol[:, 1:2], ALU.pow).then_inc(s_pow, 1)

            def take_index(s):
                pool.tensor_copy(idx[:, :].rearrange("p (n c) -> p n c", n=NGRAMS),
                                 ids[:, :, bass.ds(s * CHUNKS, CHUNKS)]).then_inc(s_idx, 1)

            def gather(g):
                n, c = divmod(g, CHUNKS)
                pool.indirect_dma_start(gath[:, n, c, :], None, emb[n],
                                        bass.IndirectOffsetOnAxis(ap=idx[:, g:g + 1], axis=0)).then_inc(s_gath, 16)

            def norm_scale(value):
                wait_step(s_mom, value)
                pool.tensor_scalar(var_eps[:, :], moments[:, :, 1], EPS, None, ALU.add).then_inc(s_var, 1)
                pool.wait_ge(s_var, value)
                pool.tensor_tensor(rstd[:, :], var_eps[:, :], minus_half[:, :], ALU.pow).then_inc(s_rstd, 1)

            def decayed_input(value):
                wait_step(s_xn, value)
                pool.tensor_scalar(xn_in[:, :, :], xn[:, 1:CHUNKS, :], decay_in[:, 0:1], None,
                                   ALU.mult).then_inc(s_xn_in, 1)

            def x_low(par, k):
                wait_step(s_x_hi, k)
                pool.tensor_tensor(x_lo[:, par, :], xn_t[:, :], x_hi[:, par, :].bitcast(F32),
                                   ALU.subtract).then_inc(s_x_lo, 1)

            def hidden_low(q, u):
                pool.wait_ge(s_hid_hi, u + 1)
                pool.tensor_tensor(hid_lo[:, hbuf_of(q), :], hid[:, q % 2, :],
                                   hid_hi[:, hbuf_of(q), :].bitcast(F32), ALU.subtract).then_inc(s_hid_lo, 1)

            pool.wait_ge(s_ids, 1)
            take_index(0)
            pool.wait_ge(s_idx, 1)
            for g in range(GATHERS):
                gather(g)
            pool.wait_ge(s_power, 1)
            pool.affine_select(out=decay_mask, in_=decay_mask, compare_op=ALU.is_gt, fill=0.0,
                               base=0, pattern=[[-1, P]], channel_multiplier=1).then_inc(s_pow, 1)

            pool.wait_ge(s_gath, 16 * GATHERS)
            take_index(1)
            pool.wait_ge(s_idx, 2)
            pool.wait_ge(s_emb_ps, NGRAMS)
            norm_scale(1)
            decayed_input(1)
            for g in range(GATHERS):
                gather(g)
            norm_scale(2)
            x_low(0, 1)
            for q in range(LEAD - 1):
                hidden_low(q, q)

            with pool.Fori(0, SEQS) as i:
                nxt = pool.snap((i + 1) % 2)
                tile0 = pool.snap(i * TILES)
                for p in range(TILES):
                    if p == INDEX:
                        wait_step(s_gath, i * (16 * GATHERS) + 2 * 16 * GATHERS)
                        take_index(i + 2)
                    if p == EMBED_P + 2:
                        norm_scale(i * 2 + 3)
                    if p == XNT_1:
                        decayed_input(i * 2 + 3)
                    if p == PROJECT + 2:
                        norm_scale(i * 2 + 4)
                    if p == XNT_2 + 2:
                        x_low(nxt, i + 2)
                    hidden_low(tile_of(p - 1)[1], tile0 + (p + LEAD - 1))
                    if p == GATHER[0]:
                        wait_step(s_idx, i + 3)
                        wait_step(s_emb_ps, i * NGRAMS + 2 * NGRAMS)
                    if p in GATHER:
                        gather(GATHER.index(p))
            pool.wait_ge(s_gath, 16 * GATHERS * (SEQS + 2))

        @block.scalar
        def _(act):
            def wait_step(semaphore, value):
                act.wait_ge(semaphore, value)
                act.sem_inc(steps["act"], 1)

            def emb_out(n, ps, value):
                first, end = VALID[n]
                act.wait_ge(s_emb_ps, value)
                act.activation(emb_t[:, n, first:end], ps[:, first:end], ACT.Copy).then_inc(s_emb_act, 1)

            def copy_out(dst, src, ready, k, done):
                act.wait_ge(ready, k)
                act.activation(dst, src, ACT.Copy).then_inc(done, 1)

            def x_high(par, k):
                wait_step(s_xnt2, k)
                act.activation(x_hi[:, par, :], xn_t[:, :], ACT.Copy).then_inc(s_x_hi, 1)

            def exponents(k):
                act.wait_ge(s_shift, k)
                act.activation(expo[:, :, :], expo[:, :, :], ACT.Exp).then_inc(s_exp, 1)

            def comb_out(k):
                act.wait_ge(s_combt_ps, k)
                act.activation(comb_t[:, :], ps_a[0:EXPERTS, :], ACT.Copy).then_inc(s_combt, 1)

            def split_high(n):
                high = blocks[n][0]
                b = stage_of[n]
                act.wait_ge(s_stage[b], 16 * (before[n] + 1))
                act.activation(high, stage[b][:, 0:high.shape[-1]], ACT.Copy).then_inc(s_split_hi, 1)

            def gate_silu(q, u):
                act.wait_ge(s_gate_ps, u + 1)
                if not isinstance(u, int) or u >= 2:
                    act.wait_ge(s_product, u - 1)
                act.activation(gate[:, q % 2, :], ps_gate[:, q % 2, :], ACT.Silu).then_inc(s_gate, 1)

            def hidden_high(q, u, hid_count):
                if q < ROUTED:
                    act.wait_ge(s_hid, hid_count)
                else:
                    act.wait_ge(s_product, u + 1)
                act.wait_ge(s_down, u + 1)
                act.activation(hid_hi[:, hbuf_of(q), :], hid[:, q % 2, :], ACT.Copy).then_inc(s_hid_hi, 1)

            act.sem_inc(s_y_free, 1)
            for n in range(EARLY):
                split_high(n)
            act.wait_ge(s_ident, 3)
            emb_out(0, ps_a, 1)
            emb_out(2, ps_c, 3)
            split_high(EARLY)
            split_high(EARLY + 1)
            copy_out(xn_t[:, :], ps_a[:, :], s_xnt1_ps, 1, s_xnt1)
            copy_out(keyed_t[:, :], ps_b[:, :], s_key_ps, 1, s_key)
            split_high(EARLY + 2)
            copy_out(keyed_t[:, :], ps_a[:, :], s_got_ps, 1, s_got)
            split_high(EARLY + 3)
            split_high(EARLY + 4)
            copy_out(xn_t[:, :], ps_a[:, :], s_xnt2_ps, 1, s_xnt2)
            x_high(0, 1)
            exponents(1)
            comb_out(1)
            for q in range(LEAD):
                gate_silu(q, q)
                if q < LEAD - 1:
                    hidden_high(q, q, q + 1)

            with act.Fori(0, SEQS) as i:
                nxt = act.snap((i + 1) % 2)
                tile0 = act.snap(i * TILES)
                routed0 = act.snap(i * ROUTED)
                for p in range(TILES):
                    if p == EMBED_T[0]:
                        emb_out(0, ps_a, i * NGRAMS + (NGRAMS + 1))
                    if p == EMBED_T[2]:
                        emb_out(2, ps_c, i * NGRAMS + 2 * NGRAMS)
                    if p == XNT_1:
                        copy_out(xn_t[:, :], ps_a[:, :], s_xnt1_ps, i + 2, s_xnt1)
                    if p == KEYED:
                        copy_out(keyed_t[:, :], ps_b[:, :], s_key_ps, i + 2, s_key)
                    if p == RETRIEVE:
                        copy_out(keyed_t[:, :], ps_a[:, :], s_got_ps, i + 2, s_got)
                    if p == XNT_2:
                        copy_out(xn_t[:, :], ps_a[:, :], s_xnt2_ps, i + 2, s_xnt2)
                    if p == XNT_2 + 1:
                        x_high(nxt, i + 2)
                    if p == ROUTE + 3:
                        exponents(i + 2)
                    if p == COMB_T:
                        comb_out(i + 2)
                    if p == TILES - 1:
                        act.wait_ge(s_down, tile0 + (TILES + LEAD))
                        act.activation(y_t[:, :], ps_y[:, :], ACT.Copy).then_inc(s_y_free, 1)
                    gate_silu(tile_of(p)[1], tile0 + (p + LEAD))
                    later, q = tile_of(p - 1)
                    hidden_high(q, tile0 + (p + LEAD - 1), routed0 + (later * ROUTED + q + 1))

        @block.vector
        def _(dve):
            def modulo(dst, v, quotient, f):
                dve.drain()
                dve.tensor_scalar(quotient, v, 1.0 / VOCAB, -0.5, ALU.mult, ALU.add)
                dve.drain()
                dve.scalar_tensor_tensor(out=dst, in0=quotient, scalar=-float(VOCAB), in1=v,
                                         op0=ALU.mult, op1=ALU.add)
                dve.drain()
                dve.tensor_scalar(f, dst, float(VOCAB), -float(VOCAB), ALU.is_ge, ALU.mult)
                dve.drain()
                dve.tensor_tensor(dst, dst, f, ALU.add)
                dve.drain()

            def roll(dst, hashed, token):
                n = dst.shape[-1]
                v = tmp_f[:, 1, 0:n]
                dve.scalar_tensor_tensor(out=v, in0=hashed, scalar=BASE, in1=token, op0=ALU.mult, op1=ALU.add)
                modulo(dst, v, tmp_i[:, 0:n], tmp_f[:, 0, 0:n])

            def split_low(n):
                high, low, _ = blocks[n]
                dve.wait_ge(s_split_hi, n + 1)
                dve.tensor_tensor(low, stage[stage_of[n]][:, 0:low.shape[-1]], high.bitcast(F32),
                                  ALU.subtract).then_inc(s_split_lo, 1)

            dve.wait_ge(s_x, 48)
            dve.tensor_copy(xf[:, 0, :], xi[:, :])
            modulo(xf[:, 1, :], xf[:, 0, :], tmp_i[:, :], tmp_f[:, 0, :])
            roll(xf[:, 2, 1:W], xf[:, 1, 0:W - 1], xf[:, 0, 1:W])
            roll(xf[:, 3, 1:W - 1], xf[:, 2, 1:W - 1], xf[:, 0, 2:W])
            roll(tmp_f[:, 2, 2:W - 1], xf[:, 3, 1:W - 2], xf[:, 0, 3:W])
            dve.tensor_copy(id_f[:, 0, :], xf[:, 2, 2:P + 2])
            dve.tensor_copy(id_f[:, 1, :], xf[:, 3, 2:P + 2])
            dve.tensor_copy(id_f[:, 2, :], tmp_f[:, 2, 2:P + 2]).then_inc(s_hash, 1)
            dve.wait_ge(s_hash_ps, 1)
            dve.tensor_copy(ids[:, :, 0:P], ps_a[:, 0:NGRAMS * P].rearrange("p (n t) -> p n t", n=NGRAMS)).then_inc(s_ids, 1)

            dve.wait_ge(s_spread_ps, 1)
            dve.tensor_copy(bias[:, :], ps_b[:, 0:P])
            dve.tensor_copy(scale[:, :], ps_b[:, P + 1:P + 2])
            dve.tensor_scalar(dcol[:, 1:2], ps_b[:, P:P + 1], -1.0, None, ALU.mult).then_inc(s_spread, 1)

            split_low(0)
            split_low(1)

            dve.memset(powers[:, :], 1.0)
            dve.wait_ge(s_const, 6)
            dve.wait_ge(s_pow, 1)
            dve.tensor_scalar(decay[:, :], dcol[:, 2:3], 1.0, None, ALU.add)
            dve.drain()
            dve.reciprocal(decay[:, :], decay[:, :])
            for b in range(7):
                dve.tensor_scalar(bit, exponent, b, 1, ALU.arith_shift_right, ALU.bitwise_and)
                dve.drain()
                dve.tensor_scalar(no_bit, bit, -1.0, 1.0, ALU.mult, ALU.add)
                dve.drain()
                dve.scalar_tensor_tensor(out=powers[:, :], in0=no_bit, scalar=decay[:, 0:1], in1=powers[:, :],
                                         op0=ALU.max, op1=ALU.mult)
                dve.drain()
                dve.tensor_tensor(decay[:, :], decay[:, :], decay[:, :], ALU.mult)
            dve.drain()
            dve.tensor_copy(decay_chunk[:, :], decay[:, :]).then_inc(s_power, 1)

            dve.wait_ge(s_wt_ps, 1)
            dve.tensor_copy(w_t, ps_gate[:, 0, :].rearrange("p (a b) -> p a b", a=4)).then_inc(s_wt, 1)
            dve.wait_ge(s_av_ps, 1)
            dve.tensor_copy(qk_w[:, :], ps_gate[:, 1, 0:P])
            dve.tensor_scalar(vo_w[:, :], ps_gate[:, 1, P:2 * P], scale[:, 0:1], None, ALU.mult).then_inc(s_av, 1)

            def emb_out(value):
                first, end = VALID[1]
                dve.wait_ge(s_emb_ps, value)
                dve.tensor_copy(emb_t[:, 1, first:end], ps_b[:, first:end]).then_inc(s_emb_dve, 1)

            def half_moments(t):
                dve.drain()
                for c in range(CHUNKS):
                    dve.bn_stats(out=stats[:, c, :], in_=t[:, c, :])

            def moments_of():
                dve.drain()
                for c in range(CHUNKS):
                    last = dve.bn_aggr(out=moments[:, c, :], in_=stats[:, c, :])
                last.then_inc(s_mom, 1)

            def embedded(k):
                dve.wait_ge(s_h1_ps, k)
                dve.tensor_tensor(h1[:, :, :], chunked(ps_b), bias[:, None, :].to_broadcast([P, CHUNKS, P]), ALU.add)

            def normalise(t, first, value):
                dve.wait_ge(s_rstd, value)
                for c in (first, first + 1):
                    last = dve.tensor_scalar(xn[:, c, :], t[:, c, :], moments[:, c, 0:1], rstd[:, c:c + 1],
                                             ALU.subtract, ALU.mult)
                if first:
                    last.then_inc(s_xn, 1)

            def key_decayed(k):
                dve.wait_ge(s_key, k)
                dve.tensor_tensor(keyed_out[:, :, :], chunked(keyed_t)[:, 0:CHUNKS - 1, :],
                                  decay_out[:, None, :].to_broadcast([P, CHUNKS - 1, P]),
                                  ALU.mult).then_inc(s_key_out, 1)

            def mask_scores(k):
                dve.wait_ge(s_score_ps, k)
                dve.tensor_tensor(scores[:, :, :], chunked(ps_a), decay_mask[:, None, :].to_broadcast([P, CHUNKS, P]),
                                  ALU.mult).then_inc(s_score, 1)

            def chain_states(k):
                dve.wait_ge(s_state_ps, k)
                last = dve.tensor_copy(state[:, CHUNKS - 2, :], ps_b[:, (CHUNKS - 2) * P:(CHUNKS - 1) * P])
                for j in range(CHUNKS - 3, -1, -1):
                    dve.drain()
                    last = dve.scalar_tensor_tensor(out=state[:, j, :], in0=state[:, j + 1, :],
                                                    scalar=decay_chunk[:, 0:1], in1=ps_b[:, j * P:(j + 1) * P],
                                                    op0=ALU.mult, op1=ALU.add)
                last.then_inc(s_state, 1)

            def half(t, par):
                return t[:, par, :].rearrange("p (c n) -> p c n", c=CHUNKS)

            def attended(par, k):
                dve.wait_ge(s_h2_ps, k)
                dve.tensor_tensor(half(h2, par), chunked(ps_b), h1[:, :, :], ALU.add)

            def take_logits(k):
                dve.wait_ge(s_route_ps, k)
                dve.tensor_copy(logits[:, :, :], ps_b[:, 0:CHUNKS * EXPERTS].rearrange("p (c e) -> p c e", c=CHUNKS))\
                   .then_inc(s_logits, 1)

            def sort_top():
                dve.drain()
                for c in range(CHUNKS):
                    dve.max(top[:, c, :], logits[:, c, :])

            def shift():
                dve.drain()
                dve.tensor_tensor(expo[:, :, :], logits[:, :, :],
                                  top[:, :, 0:1].to_broadcast([P, CHUNKS, EXPERTS]), ALU.subtract).then_inc(s_shift, 1)
                dve.memset(top[:, :, TOP_K:8], -HUGE)

            def strike_top():
                dve.drain()
                for c in range(CHUNKS):
                    dve.match_replace(out=struck[:, c, :], in_to_replace=top[:, c, :], in_values=logits[:, c, :],
                                      imm_value=-HUGE)

            def choose(k):
                dve.drain()
                dve.tensor_tensor(struck[:, :, :], struck[:, :, :], logits[:, :, :], ALU.not_equal)
                dve.drain()
                dve.wait_ge(s_exp, k)
                dve.tensor_tensor(struck[:, :, :], struck[:, :, :], expo[:, :, :], ALU.mult)

            def weigh():
                dve.drain()
                dve.tensor_reduce(total[:, :], struck[:, :, :], AX_X, ALU.add)
                dve.drain()
                dve.reciprocal(inv_total[:, :], total[:, :])
                dve.drain()
                dve.tensor_tensor(struck[:, :, :], struck[:, :, :],
                                  inv_total[:, :, None].to_broadcast([P, CHUNKS, EXPERTS]), ALU.mult).then_inc(s_comb, 1)

            def hidden(q, u, hid_count, spread_count):
                if not isinstance(u, int) or u >= 2:
                    dve.wait_ge(s_hid_lo, u - 1)
                dve.wait_ge(s_gate, u + 1)
                dve.wait_ge(s_lin_ps, u + 1)
                dst = product if q < ROUTED else hid
                dve.tensor_tensor(dst[:, q % 2, :], gate[:, q % 2, :], ps_lin[:, q % 2, :], ALU.mult).then_inc(s_product, 1)
                if q < ROUTED:
                    dve.drain()
                    dve.wait_ge(s_spread_w[q % COMB_BUFS], spread_count)
                    dve.tensor_tensor(hid[:, q % 2, :], product[:, q % 2, :], spread[:, q % COMB_BUFS, :],
                                      ALU.mult).then_inc(s_hid, 1)

            for n in range(2, EARLY):
                split_low(n)
            emb_out(2)
            embedded(1)
            half_moments(h1)
            moments_of()
            split_low(EARLY)
            normalise(h1, 0, 1)
            normalise(h1, 2, 1)
            split_low(EARLY + 1)
            key_decayed(1)
            dve.wait_ge(s_pow, 2)
            mask_scores(1)
            chain_states(1)
            split_low(EARLY + 2)
            attended(0, 1)
            half_moments(half(h2, 0))
            moments_of()
            split_low(EARLY + 3)
            normalise(half(h2, 0), 0, 2)
            normalise(half(h2, 0), 2, 2)
            split_low(EARLY + 4)
            take_logits(1)
            sort_top()
            shift()
            strike_top()
            choose(1)
            weigh()
            for q in range(LEAD):
                hidden(q, q, q + 1, 16)
            dve.sem_inc(s_res, 1)

            with dve.Fori(0, SEQS) as i:
                cur = dve.snap(i % 2)
                nxt = dve.snap((i + 1) % 2)
                tile0 = dve.snap(i * TILES)
                routed0 = dve.snap(i * ROUTED)
                spread0 = dve.snap(i * (16 * ROUTED // COMB_BUFS))
                for p in range(TILES):
                    if p == EMBED_T[1]:
                        emb_out(i * NGRAMS + (NGRAMS + 2))
                    if p == EMBED_P:
                        embedded(i + 2)
                    if p == EMBED_P + 1:
                        half_moments(h1)
                    if p == EMBED_P + 2:
                        moments_of()
                    if p == EMBED_P + 3:
                        normalise(h1, 0, i * 2 + 3)
                    if p == EMBED_P + 4:
                        normalise(h1, 2, i * 2 + 3)
                    if p == KEYED + 1:
                        key_decayed(i + 2)
                    if p == SCORE + 1:
                        mask_scores(i + 2)
                    if p == STATE + 1:
                        chain_states(i + 2)
                    if p == PROJECT:
                        attended(nxt, i + 2)
                    if p == PROJECT + 1:
                        half_moments(half(h2, nxt))
                    if p == PROJECT + 2:
                        moments_of()
                    if p == PROJECT + 3:
                        normalise(half(h2, nxt), 0, i * 2 + 4)
                    if p == PROJECT + 4:
                        normalise(half(h2, nxt), 2, i * 2 + 4)
                    if p == ROUTE:
                        take_logits(i + 2)
                    if p == ROUTE + 1:
                        sort_top()
                    if p == ROUTE + 2:
                        shift()
                    if p == ROUTE + 3:
                        strike_top()
                    if p == ROUTE + 4:
                        choose(i + 2)
                    if p == ROUTE + 5:
                        weigh()
                    later, q = tile_of(p)
                    hidden(q, tile0 + (p + LEAD), routed0 + (later * ROUTED + q + 1),
                           spread0 + 16 * ((later * ROUTED + q) // COMB_BUFS + 1))
                dve.wait_ge(s_res_ps, i + 1)
                dve.tensor_tensor(result[:, :, :], chunked(ps_c), half(h2, cur), ALU.add).then_inc(s_res, 1)

        @block.tensor
        def _(pe):
            def chunk(t, c):
                return t[:, c * P:(c + 1) * P]

            def transposes(dst, parts, signal):
                for c, part in enumerate(parts):
                    last = pe.transpose(chunk(dst, c), part, ident[:, :])
                last.then_inc(signal, 1)

            pe.wait_ge(s_ident, 2)
            pe.wait_ge(s_hash, 1)
            transposes(ps_a, [id_f[:, n, :] for n in range(NGRAMS)], s_hash_ps)
            pe.wait_ge(s_row, 16)
            pe.matmul(ps_b[:, 0:P + 2], ones_row[:, :], row[:, :], start=True, stop=True).then_inc(s_spread_ps, 1)
            pe.wait_ge(s_small, 64)
            for m in range(4):
                last = pe.matmul(ps_gate[:, 0, m * P:(m + 1) * P], small_w[:, 1 + m, :], small_w[:, 0, :],
                                 start=True, stop=True)
            last.then_inc(s_wt_ps, 1)
            pe.wait_ge(s_wt, 1)
            for m in range(2):
                last = pe.matmul(ps_gate[:, 1, m * P:(m + 1) * P], w_t[:, 2 * m, :], w_t[:, 2 * m + 1, :],
                                 start=True, stop=True)
            last.then_inc(s_av_ps, 1)

            def embed_t(n):
                transposes((ps_a, ps_b, ps_c)[n], [gath[:, n, c, :] for c in range(CHUNKS)], s_emb_ps)

            def embed_project():
                for c in range(CHUNKS):
                    for n in range(NGRAMS):
                        last = pe.matmul(chunk(ps_b, c), emb_t[:, n, c * P:(c + 1) * P], proj[:, n, :],
                                         start=(n == 0), stop=(n == NGRAMS - 1))
                last.then_inc(s_h1_ps, 1)

            def xn_transpose(value, signal):
                pe.wait_ge(s_xn, value)
                transposes(ps_a, [xn[:, c, :] for c in range(CHUNKS)], signal)

            def keyed(k):
                pe.wait_ge(s_xnt1, k)
                pe.matmul(ps_b[:, :], qk_w[:, :], xn_t[:, :], start=True, stop=True).then_inc(s_key_ps, 1)

            def score(k):
                pe.wait_ge(s_key, k)
                for c in range(CHUNKS):
                    last = pe.matmul(chunk(ps_a, c), chunk(xn_t, c), chunk(keyed_t, c), start=True, stop=True)
                last.then_inc(s_score_ps, 1)

            def chunk_sums(k):
                pe.wait_ge(s_xn_in, k)
                for j in range(CHUNKS - 1):
                    last = pe.matmul(chunk(ps_b, j), xn_in[:, j, :], xn[:, j + 1, :], start=True, stop=True)
                last.then_inc(s_state_ps, 1)

            def retrieve(k):
                pe.wait_ge(s_score, k)
                pe.wait_ge(s_state, k)
                pe.wait_ge(s_key_out, k)
                for c in range(CHUNKS):
                    last = pe.matmul(chunk(ps_a, c), xn[:, c, :], scores[:, c, :], start=True, stop=(c == CHUNKS - 1))
                    if c < CHUNKS - 1:
                        last = pe.matmul(chunk(ps_a, c), state[:, c, :], keyed_out[:, c, :], start=False, stop=True)
                last.then_inc(s_got_ps, 1)

            def project(k):
                pe.wait_ge(s_got, k)
                for c in range(CHUNKS):
                    last = pe.matmul(chunk(ps_b, c), chunk(keyed_t, c), vo_w[:, :], start=True, stop=True)
                last.then_inc(s_h2_ps, 1)

            def route(k):
                pe.wait_ge(s_xnt2, k)
                for c in range(CHUNKS):
                    last = pe.matmul(ps_b[:, c * EXPERTS:(c + 1) * EXPERTS], chunk(xn_t, c), wg[:, :],
                                     start=True, stop=True)
                last.then_inc(s_route_ps, 1)

            def comb_transpose(k):
                pe.wait_ge(s_comb, k)
                pe.sem_inc(steps["pe"], 1)
                for c in range(CHUNKS):
                    last = pe.transpose(chunk(ps_a, c)[0:EXPERTS, :], struck[:, c, :], ident[:, :])
                last.then_inc(s_combt_ps, 1)

            def up(q, par, u):
                cols = slice(q * P, (q + 1) * P)
                for m, (ps, used, signal) in enumerate(((ps_gate, s_gate, s_gate_ps), (ps_lin, s_product, s_lin_ps))):
                    if not isinstance(u, int) or u >= 2:
                        pe.wait_ge(used, u - 1)
                    dst = ps[:, q % 2, :]
                    pe.matmul(dst, up_hi[:, m, cols], x_hi[:, par, :], start=True, stop=False)
                    pe.matmul(dst, up_hi[:, m, cols], x_lo[:, par, :], start=False, stop=False)
                    pe.matmul(dst, up_lo[:, m, cols], x_hi[:, par, :], start=False, stop=True).then_inc(signal, 1)

            def down_tile(q, u):
                cols = slice(q * P, (q + 1) * P)
                pe.wait_ge(s_hid_lo, u + 1)
                pe.matmul(ps_y[:, :], down_hi[:, cols], hid_hi[:, hbuf_of(q), :], start=(q == 0), stop=False)
                pe.matmul(ps_y[:, :], down_hi[:, cols], hid_lo[:, hbuf_of(q), :], start=False, stop=False)
                pe.matmul(ps_y[:, :], down_lo[:, cols], hid_hi[:, hbuf_of(q), :], start=False,
                          stop=(q == TILES - 1)).then_inc(s_down, 1)

            pe.wait_ge(s_gath, 16 * GATHERS)
            embed_t(0)
            pe.wait_ge(s_spread, 1)
            embed_t(1)
            embed_t(2)
            pe.wait_ge(s_emb_act, 2)
            pe.wait_ge(s_emb_dve, 1)
            embed_project()
            xn_transpose(1, s_xnt1_ps)
            pe.wait_ge(s_av, 1)
            keyed(1)
            score(1)
            chunk_sums(1)
            retrieve(1)
            project(1)
            xn_transpose(2, s_xnt2_ps)
            route(1)
            comb_transpose(1)
            pe.wait_ge(s_split_lo, len(blocks))
            pe.wait_ge(s_x_lo, 1)
            pe.sem_inc(s_down, LEAD)
            for q in range(LEAD):
                up(q, 0, q)

            with pe.Fori(0, SEQS) as i:
                cur = pe.snap(i % 2)
                nxt = pe.snap((i + 1) % 2)
                tile0 = pe.snap(i * TILES)
                for p in range(TILES):
                    if p == EMBED_T[0]:
                        pe.wait_ge(s_gath, i * (16 * GATHERS) + 2 * 16 * GATHERS)
                        pe.wait_ge(s_combt, i + 1)
                        embed_t(0)
                    if p == EMBED_T[1]:
                        pe.wait_ge(s_logits, i + 1)
                        embed_t(1)
                    if p == EMBED_T[2]:
                        pe.wait_ge(s_res, i + 1)
                        embed_t(2)
                    if p == EMBED_P:
                        pe.wait_ge(s_emb_act, i * 2 + 4)
                        pe.wait_ge(s_emb_dve, i + 2)
                        embed_project()
                    if p == XNT_1:
                        xn_transpose(i * 2 + 3, s_xnt1_ps)
                    if p == KEYED:
                        keyed(i + 2)
                    if p == SCORE:
                        score(i + 2)
                    if p == STATE:
                        chunk_sums(i + 2)
                    if p == RETRIEVE:
                        retrieve(i + 2)
                    if p == PROJECT:
                        project(i + 2)
                    if p == XNT_2:
                        xn_transpose(i * 2 + 4, s_xnt2_ps)
                    if p == ROUTE:
                        route(i + 2)
                    if p == COMB_T:
                        comb_transpose(i + 2)
                    if p == 0:
                        pe.wait_ge(s_y_free, i + 1)
                    later, q = tile_of(p)
                    if p == TILES - 1:
                        down_tile(p, tile0 + p)
                    if later and q == 0:
                        pe.wait_ge(s_x_lo, i + 2)
                    up(q, nxt if later else cur, tile0 + (p + LEAD))
                    if p < TILES - 1:
                        down_tile(p, tile0 + p)
                pe.wait_ge(s_y_free, i + 2)
                transposes(ps_c, [chunk(y_t, c) for c in range(CHUNKS)], s_res_ps)


def kernel(**inputs):
    import concourse.bacc as bacc
    from concourse.bass_utils import run_bass_kernel_spmd

    nc = bacc.Bacc("TRN2", target_bir_lowering=False, num_devices=1)
    a = {k: np.asarray(v) for k, v in inputs.items()}

    def interleaved(name):
        return a[name].reshape(ROUTED, 2, INTER, P).transpose(0, 2, 1, 3).reshape(EXPERTS * INTER, P)

    def hidden_major(name, shared):
        return np.concatenate([interleaved(name), a[shared]], axis=0).T

    down = np.concatenate([interleaved("L0_ffn_w2"), a["L0_ffn_w_sd"].T], axis=0)
    arrays = {
        "x": a["x"].reshape(P, P),
        "emb_2": a["L0_tok_emb_2"], "emb_3": a["L0_tok_emb_3"], "emb_4": a["L0_tok_emb_4"],
        "proj_t": a["L0_tok_proj_w"].T.reshape(NGRAMS, P, P).transpose(1, 0, 2),
        "rows": np.concatenate([a["L0_tok_proj_b"].reshape(1, P), a["L0_attn_decay_logit"].reshape(1, 1),
                                a["L0_attn_out_scale"].reshape(1, 1)], axis=1),
        "basis_t": a["L0_attn_basis"].T,
        "coeff_t": np.stack([a[f"L0_attn_{m}_coeffs"].T for m in "qkvo"], axis=1),
        "wg_t": a["L0_ffn_w_gate"].T,
        "up_gate": hidden_major("L0_ffn_w1", "L0_ffn_w_sg"),
        "up_lin": hidden_major("L0_ffn_w3", "L0_ffn_w_su"),
        "down": down.reshape(TILES, P, P).transpose(1, 0, 2).reshape(P, TILES * P),
    }
    arrays = {k: np.ascontiguousarray(v) for k, v in arrays.items()}
    ap = {k: nc.dram_tensor(k, v.shape, mybir.dt.from_np(v.dtype), kind="ExternalInput").ap()
          for k, v in arrays.items()}
    out = nc.dram_tensor("out", (SEQS, SEQ_LEN, P), F32, kind="ExternalOutput").ap()
    comb_dram = nc.dram_tensor("comb_dram", (2, EXPERTS, SEQ_LEN), F32, kind="Internal").ap()
    build(nc, ap["x"], [ap["emb_2"], ap["emb_3"], ap["emb_4"]], ap["proj_t"], ap["rows"], ap["basis_t"],
          ap["coeff_t"], ap["wg_t"], ap["up_gate"], ap["up_lin"], ap["down"],
          comb_dram, out.rearrange("s (c p) d -> s p c d", c=CHUNKS))
    return run_bass_kernel_spmd(nc, [arrays], core_ids=[0]).results[0]["out"]
```

```python
from contextlib import ExitStack

import concourse.bass as bass
import numpy as np
from concourse import mybir

ALU = mybir.AluOpType
ACT = mybir.ActivationFunctionType
AX_X = mybir.AxisListType.X
F32 = mybir.dt.float32
F32R = mybir.dt.float32r
I32 = mybir.dt.int32
U32 = mybir.dt.uint32

P = 128
SEQS, SEQ_LEN = 32, 512
CHUNKS = SEQ_LEN // P
VOCAB, BASE = 25000, 64.0
NGRAMS = 3
EXPERTS, INTER, TOP_K = 64, 64, 6
ROUTED = EXPERTS * INTER // P
SHARED = 256 // P
TILES = ROUTED + SHARED
BLOCK = 12
LEAD = 3
POWERS = 2 * P + 1
EPS = 1e-5
HUGE = 3e38
E_NUMBER = float(np.e)

VALID = [(1, SEQ_LEN), (1, SEQ_LEN - 1), (2, SEQ_LEN - 1)]

EMBED_T = (0, 0, 1)
EMBED_P = 2
XNT_1 = 8
KEYED = 9
STATE = 10
SCORE = 10
RETRIEVE = 13
PROJECT = 14
XNT_2 = 20
ROUTE = 21
COMB_T = 28
INDEX = 3
GATHER = (4, 6, 8, 10, 12, 14, 18, 20, 22, 24, 26, 28)
AHEAD = 2
COMB_BUFS = 8


def hbuf_of(q):
    return 3 if q == TILES - 1 else q % 3


def build(nc, x, emb, proj_t, rows, basis_t, coeff_t, wg_t, up_gate, up_lin, down, comb_dram, out):
    ctx = ExitStack()
    with ctx:
        def sb(name, shape, dt=F32):
            return ctx.enter_context(nc.sbuf_tensor(name, shape, dt))

        def pb(name, shape, dt=F32):
            return ctx.enter_context(nc.psum_tensor(name, shape, dt))

        def sem(name):
            return ctx.enter_context(nc.semaphore(name))

        up_hi = sb("up_hi", [P, 2, TILES * P], F32R)
        up_lo = sb("up_lo", [P, 2, TILES * P], F32R)
        down_hi = sb("down_hi", [P, TILES * P], F32R)
        down_lo = sb("down_lo", [P, TILES * P], F32R)
        proj = sb("proj", [P, NGRAMS, P])
        wg = sb("wg", [P, EXPERTS])
        qk_w = sb("qk_w", [P, P])
        vo_w = sb("vo_w", [P, P])
        ident = sb("ident", [P, P])
        bias = sb("bias", [P, P])
        powers = sb("powers", [P, POWERS])
        decay_mask = powers[:, 0:P]
        decay_out = powers[:, P:2 * P]
        decay_in = powers[:, 2 * P:2 * P + 1]
        decay_chunk = sb("decay_chunk", [P, 1])
        decay = sb("decay", [P, 1])
        scale = sb("scale", [P, 1])
        minus_half = sb("minus_half", [P, CHUNKS])
        ids = sb("ids", [P, NGRAMS, (SEQS + 1) * CHUNKS], U32)

        row = sb("row", [1, P + 2])
        ones_row = sb("ones_row", [1, P])
        xi = sb("xi", [P, P + 3], I32)
        tmp_i = sb("tmp_i", [P, P + 3], I32)
        dcol = sb("dcol", [P, 3])

        idx = sb("idx", [P, NGRAMS * CHUNKS], U32)
        gath = sb("gath", [P, NGRAMS, CHUNKS, P])
        emb_t = sb("emb_t", [P, NGRAMS, SEQ_LEN])
        h1 = sb("h1", [P, CHUNKS, P])
        stats = sb("stats", [P, CHUNKS, 6])
        moments = sb("moments", [P, CHUNKS, 2])
        var_eps = sb("var_eps", [P, CHUNKS])
        rstd = sb("rstd", [P, CHUNKS])
        xn = sb("xn", [P, CHUNKS, P])
        xn_t = sb("xn_t", [P, SEQ_LEN])
        keyed_t = sb("keyed_t", [P, SEQ_LEN])
        attention = sb("attention", [P, (4 * CHUNKS - 3) * P])
        keyed_out, xn_in, state, scores = (
            attention[:, n * (CHUNKS - 1) * P:end * P].rearrange("p (c n) -> p c n", n=P)
            for n, end in enumerate((CHUNKS - 1, 2 * (CHUNKS - 1), 3 * (CHUNKS - 1), 4 * CHUNKS - 3)))
        logits = sb("logits", [P, CHUNKS, EXPERTS])
        top = sb("top", [P, CHUNKS, 8])
        struck = sb("struck", [P, CHUNKS, EXPERTS])
        expo = sb("expo", [P, CHUNKS, EXPERTS])
        total = sb("total", [P, CHUNKS])
        inv_total = sb("inv_total", [P, CHUNKS])
        comb_t = sb("comb_t", [EXPERTS, SEQ_LEN])

        h2 = sb("h2", [P, 2, SEQ_LEN])
        x_hi = sb("x_hi", [P, 2, SEQ_LEN], F32R)
        x_lo = sb("x_lo", [P, 2, SEQ_LEN], F32R)

        spread = sb("spread", [P, COMB_BUFS, SEQ_LEN])
        work = sb("work", [P, 8 * SEQ_LEN])
        gate = work[:, 0:2 * SEQ_LEN].rearrange("p (a t) -> p a t", a=2)
        product = work[:, 2 * SEQ_LEN:4 * SEQ_LEN].rearrange("p (a t) -> p a t", a=2)
        hid = work[:, 4 * SEQ_LEN:6 * SEQ_LEN].rearrange("p (a t) -> p a t", a=2)
        y_t = work[:, 6 * SEQ_LEN:7 * SEQ_LEN]
        result = work[:, 7 * SEQ_LEN:8 * SEQ_LEN].rearrange("p (c d) -> p c d", c=CHUNKS)
        hid_hi = sb("hid_hi", [P, 4, SEQ_LEN], F32R)
        hid_lo = sb("hid_lo", [P, 4, SEQ_LEN], F32R)

        ps_gate = pb("ps_gate", [P, 2, SEQ_LEN])
        ps_lin = pb("ps_lin", [P, 2, SEQ_LEN])
        ps_y = pb("ps_y", [P, SEQ_LEN])
        ps_a = pb("ps_a", [P, SEQ_LEN])
        ps_b = pb("ps_b", [P, SEQ_LEN])
        ps_c = pb("ps_c", [P, SEQ_LEN])

        def chunked(t):
            return t[:, :].rearrange("p (c n) -> p c n", c=CHUNKS)

        stage = [work[:, 0:BLOCK * P], work[:, BLOCK * P:2 * BLOCK * P]]
        stage.append(attention[:, 0:BLOCK * P])
        spread_flat = spread[:, :, :].rearrange("p a t -> p (a t)")
        small_w = spread_flat[:, 0:5 * P].rearrange("p (a b) -> p a b", a=5)
        w_t = spread_flat[:, 5 * P:9 * P].rearrange("p (a b) -> p a b", a=4)
        exponent = spread_flat[:, 9 * P:9 * P + POWERS].bitcast(I32)
        bit = spread_flat[:, 9 * P + POWERS:9 * P + 2 * POWERS].bitcast(I32)
        no_bit = spread_flat[:, 9 * P + 2 * POWERS:9 * P + 3 * POWERS]
        W = P + 3
        xf = work[:, 2 * BLOCK * P:2 * BLOCK * P + 4 * W].rearrange("p (a t) -> p a t", a=4)
        tmp_f = work[:, 2 * BLOCK * P + 4 * W:2 * BLOCK * P + 7 * W].rearrange("p (a t) -> p a t", a=3)
        id_f = h1[:, 0:NGRAMS, :]

        s_xi = sem("s_xi")
        s_x = sem("s_x")
        s_small = sem("s_small")
        s_row = sem("s_row")
        s_stage = [sem(f"s_stage{b}") for b in range(len(stage))]
        s_split_hi = sem("s_split_hi")
        s_split_lo = sem("s_split_lo")
        s_const = sem("s_const")
        s_ident = sem("s_ident")
        s_pow = sem("s_pow")
        s_spread_ps = sem("s_spread_ps")
        s_spread = sem("s_spread")
        s_power = sem("s_power")
        s_hash = sem("s_hash")
        s_hash_ps = sem("s_hash_ps")
        s_ids = sem("s_ids")
        s_wt_ps = sem("s_wt_ps")
        s_wt = sem("s_wt")
        s_av_ps = sem("s_av_ps")
        s_av = sem("s_av")
        steps = {e: sem("steps_" + e) for e in ("pool", "act", "sp", "pe")}
        s_idx = sem("s_idx")
        s_gath = [sem(f"s_gath{n}") for n in range(NGRAMS)]
        s_emb_ps = sem("s_emb_ps")
        s_emb_act = sem("s_emb_act")
        s_emb_dve = sem("s_emb_dve")
        s_h1_ps = sem("s_h1_ps")
        s_mom = sem("s_mom")
        s_var = sem("s_var")
        s_rstd = sem("s_rstd")
        s_xn = sem("s_xn")
        s_xn_in = sem("s_xn_in")
        s_xnt1_ps = sem("s_xnt1_ps")
        s_xnt1 = sem("s_xnt1")
        s_key_ps = sem("s_key_ps")
        s_key = sem("s_key")
        s_key_out = sem("s_key_out")
        s_score_ps = sem("s_score_ps")
        s_score = sem("s_score")
        s_state_ps = sem("s_state_ps")
        s_state = sem("s_state")
        s_got_ps = sem("s_got_ps")
        s_got = sem("s_got")
        s_h2_ps = sem("s_h2_ps")
        s_xnt2_ps = sem("s_xnt2_ps")
        s_xnt2 = sem("s_xnt2")
        s_x_hi = sem("s_x_hi")
        s_x_lo = sem("s_x_lo")
        s_route_ps = sem("s_route_ps")
        s_logits = sem("s_logits")
        s_shift = sem("s_shift")
        s_exp = sem("s_exp")
        s_comb = sem("s_comb")
        s_combt_ps = sem("s_combt_ps")
        s_combt = sem("s_combt")
        s_y_free = sem("s_y_free")
        s_res_ps = sem("s_res_ps")
        s_res = sem("s_res")
        s_stored = sem("s_stored")
        s_spread_w = [sem(f"s_spread_w{b}") for b in range(COMB_BUFS)]
        s_gate_ps = sem("s_gate_ps")
        s_lin_ps = sem("s_lin_ps")
        s_gate = sem("s_gate")
        s_product = sem("s_product")
        s_hid = sem("s_hid")
        s_hid_hi = sem("s_hid_hi")
        s_hid_lo = sem("s_hid_lo")
        s_down = sem("s_down")

        block = ctx.enter_context(nc.Block())

        blocks = []
        for first in range(0, TILES, BLOCK):
            cols = slice(first * P, min(first + BLOCK, TILES) * P)
            for k, src in enumerate((up_gate, up_lin)):
                blocks.append((up_hi[:, k, cols], up_lo[:, k, cols], src[:, cols]))
            blocks.append((down_hi[:, cols], down_lo[:, cols], down[:, cols]))

        stage_of = [n if n < 3 else (n + 1) % 2 for n in range(len(blocks))]
        before = [stage_of[:n].count(b) for n, b in enumerate(stage_of)]

        GATHERS = NGRAMS * CHUNKS

        def held(engine, value):
            return value if isinstance(value, int) else engine.snap(value)

        def tile_of(p):
            return (p + LEAD) // TILES, (p + LEAD) % TILES


        @block.sync
        def _(sp):
            sp.wait_ge(s_xi, 1)
            sp.dma_start(xi[:, 2:P + 2], x).then_inc(s_x, 16)
            sp.dma_start(xi[1:P, 0:2], x[0:P - 1, P - 2:P]).then_inc(s_x, 16)
            sp.dma_start(xi[0:P - 1, P + 2:P + 3], x[1:P, 0:1], allow_slow_non_contiguous=True).then_inc(s_x, 16)
            sp.dma_start(row[:, :], rows).then_inc(s_row, 16)
            sp.dma_start(small_w[:, 0, :], basis_t).then_inc(s_small, 16)
            sp.dma_start(small_w[:, 1:5, :], coeff_t).then_inc(s_small, 16)
            sp.dma_start(proj[:, :, :], proj_t).then_inc(s_small, 16)
            sp.dma_start(wg[:, :], wg_t).then_inc(s_small, 16)
            for n, (_, _, src) in enumerate(blocks):
                b = stage_of[n]
                if before[n]:
                    last = max(m for m in range(n) if stage_of[m] == b)
                    sp.wait_ge(s_split_lo, last + 1)
                sp.dma_start(stage[b][:, 0:src.shape[-1]], src).then_inc(s_stage[b], 16)

            def load_spread(q, par):
                src = comb_dram[par, 2 * q:2 * q + 2, :]
                src = src[None, :, :].to_broadcast([INTER, 2, SEQ_LEN])
                sp.dma_start(spread[:, q % COMB_BUFS, :], src).then_inc(s_spread_w[q % COMB_BUFS], 16)

            sp.wait_ge(s_combt, 1)
            sp.dma_start(comb_dram[0, :, :], comb_t[:, :]).then_inc(s_stored, 16)
            sp.wait_ge(s_stored, 16)
            for q in range(LEAD + AHEAD):
                load_spread(q, 0)

            def sequence(i, more):
                cur = held(sp, i % 2)
                nxt = held(sp, (i + 1) % 2)
                routed0 = held(sp, i * ROUTED)
                for p in range(TILES):
                    later, q = (p + LEAD + AHEAD) // TILES, (p + LEAD + AHEAD) % TILES
                    if more and p == COMB_T + 1:
                        sp.wait_ge(s_combt, i + 2)
                        sp.sem_inc(steps["sp"], 1)
                        sp.dma_start(comb_dram[nxt, :, :], comb_t[:, :]).then_inc(s_stored, 16)
                    if more and later and q == 0:
                        sp.wait_ge(s_stored, i * 32 + 32)
                        sp.sem_inc(steps["sp"], 1)
                    if q < ROUTED and (more or not later):
                        sp.wait_ge(s_hid, routed0 + (later * ROUTED + q + 1))
                        sp.sem_inc(steps["sp"], 1)
                        load_spread(q, nxt if later else cur)
                sp.wait_ge(s_res, i + 2)
                sp.sem_inc(steps["sp"], 1)
                sp.dma_start(out[i, :, :, :], result[:, :, :]).then_inc(s_stored, 16)

            with sp.Fori(0, SEQS - 1) as i:
                sequence(i, True)
            sequence(SEQS - 1, False)
            sp.wait_ge(s_stored, 32 * SEQS)

        @block.gpsimd
        def _(pool):
            def wait_step(semaphore, value):
                pool.wait_ge(semaphore, value)
                pool.sem_inc(steps["pool"], 1)

            pool.memset(xi[:, :], 0).then_inc(s_xi, 1)
            pool.memset(ones_row[:, :], 1.0).then_inc(s_ident, 1)
            pool.memset(ident[:, :], 0.0).then_inc(s_const, 1)
            pool.wait_ge(s_const, 1)
            pool.affine_select(out=ident[:, :], in_=ident[:, :], compare_op=ALU.not_equal, fill=1.0,
                               base=0, pattern=[[-1, P]], channel_multiplier=1).then_inc(s_ident, 1)
            pool.memset(ids[:, :, SEQS * CHUNKS:], 0).then_inc(s_const, 1)
            pool.memset(minus_half[:, :], -0.5).then_inc(s_const, 1)
            pool.memset(dcol[:, 0:1], E_NUMBER).then_inc(s_const, 1)
            pool.iota(exponent[:, 0:P], [[-1, P]], base=-1, channel_multiplier=1).then_inc(s_const, 1)
            pool.iota(exponent[:, P:2 * P], [[-1, P]], base=P - 1, channel_multiplier=0).then_inc(s_const, 1)
            pool.iota(exponent[:, 2 * P:POWERS], [[0, 1]], base=0, channel_multiplier=1).then_inc(s_const, 1)
            pool.memset(emb_t[:, :, :], 0.0).then_inc(s_ident, 1)
            pool.wait_ge(s_const, 4)
            pool.wait_ge(s_spread, 1)
            pool.tensor_tensor(dcol[:, 2:3], dcol[:, 0:1], dcol[:, 1:2], ALU.pow).then_inc(s_pow, 1)

            def take_index(s):
                pool.tensor_copy(idx[:, :].rearrange("p (n c) -> p n c", n=NGRAMS),
                                 ids[:, :, bass.ds(s * CHUNKS, CHUNKS)]).then_inc(s_idx, 1)

            def gather(g):
                n, c = divmod(g, CHUNKS)
                pool.indirect_dma_start(gath[:, n, c, :], None, emb[n],
                                        bass.IndirectOffsetOnAxis(ap=idx[:, g:g + 1], axis=0)).then_inc(s_gath[n], 16)

            def norm_scale(value):
                wait_step(s_mom, value)
                pool.tensor_scalar(var_eps[:, :], moments[:, :, 1], EPS, None, ALU.add).then_inc(s_var, 1)
                pool.wait_ge(s_var, value)
                pool.tensor_tensor(rstd[:, :], var_eps[:, :], minus_half[:, :], ALU.pow).then_inc(s_rstd, 1)

            def decayed_input(value):
                wait_step(s_xn, value)
                pool.tensor_scalar(xn_in[:, :, :], xn[:, 1:CHUNKS, :], decay_in[:, 0:1], None,
                                   ALU.mult).then_inc(s_xn_in, 1)

            def x_low(par, k):
                wait_step(s_x_hi, k)
                pool.tensor_tensor(x_lo[:, par, :], xn_t[:, :], x_hi[:, par, :].bitcast(F32),
                                   ALU.subtract).then_inc(s_x_lo, 1)

            def hidden_low(q, u):
                pool.wait_ge(s_hid_hi, u + 1)
                pool.tensor_tensor(hid_lo[:, hbuf_of(q), :], hid[:, q % 2, :],
                                   hid_hi[:, hbuf_of(q), :].bitcast(F32), ALU.subtract).then_inc(s_hid_lo, 1)

            for n in range(NGRAMS):
                pool.wait_ge(s_ids, n + 1)
                pool.tensor_copy(idx[:, n * CHUNKS:(n + 1) * CHUNKS], ids[:, n, 0:CHUNKS]).then_inc(s_idx, 1)
                pool.wait_ge(s_idx, n + 1)
                for c in range(CHUNKS):
                    gather(n * CHUNKS + c)
            pool.wait_ge(s_power, 1)
            pool.affine_select(out=decay_mask, in_=decay_mask, compare_op=ALU.is_gt, fill=0.0,
                               base=0, pattern=[[-1, P]], channel_multiplier=1).then_inc(s_pow, 1)

            pool.wait_ge(s_emb_ps, NGRAMS)
            take_index(1)
            pool.wait_ge(s_idx, NGRAMS + 1)
            norm_scale(1)
            decayed_input(1)
            for g in range(GATHERS):
                gather(g)
            norm_scale(2)
            x_low(0, 1)
            for q in range(LEAD - 1):
                hidden_low(q, q)

            def sequence(i, more):
                nxt = held(pool, (i + 1) % 2)
                tile0 = held(pool, i * TILES)
                for p in range(TILES):
                    if more and p == INDEX:
                        wait_step(s_emb_ps, i * NGRAMS + 2 * NGRAMS)
                        take_index(i + 2)
                    if more and p == EMBED_P + 2:
                        norm_scale(i * 2 + 3)
                    if more and p == XNT_1:
                        decayed_input(i * 2 + 3)
                    if more and p == PROJECT + 2:
                        norm_scale(i * 2 + 4)
                    if more and p == XNT_2 + 2:
                        x_low(nxt, i + 2)
                    if more or not tile_of(p - 1)[0]:
                        hidden_low(tile_of(p - 1)[1], tile0 + (p + LEAD - 1))
                    if more and p == GATHER[0]:
                        wait_step(s_idx, i + NGRAMS + 2)
                    if more and p in GATHER:
                        gather(GATHER.index(p))

            with pool.Fori(0, SEQS - 1) as i:
                sequence(i, True)
            sequence(SEQS - 1, False)
            for n in range(NGRAMS):
                pool.wait_ge(s_gath[n], 16 * CHUNKS * (SEQS + 1))

        @block.scalar
        def _(act):
            def wait_step(semaphore, value):
                act.wait_ge(semaphore, value)
                act.sem_inc(steps["act"], 1)

            def emb_out(n, ps, value):
                first, end = VALID[n]
                act.wait_ge(s_emb_ps, value)
                act.activation(emb_t[:, n, first:end], ps[:, first:end], ACT.Copy).then_inc(s_emb_act, 1)

            def copy_out(dst, src, ready, k, done):
                act.wait_ge(ready, k)
                act.activation(dst, src, ACT.Copy).then_inc(done, 1)

            def x_high(par, k):
                wait_step(s_xnt2, k)
                act.activation(x_hi[:, par, :], xn_t[:, :], ACT.Copy).then_inc(s_x_hi, 1)

            def exponents(k):
                act.wait_ge(s_shift, k)
                act.activation(expo[:, :, :], expo[:, :, :], ACT.Exp).then_inc(s_exp, 1)

            def comb_out(k):
                act.wait_ge(s_combt_ps, k)
                act.activation(comb_t[:, :], ps_a[0:EXPERTS, :], ACT.Copy).then_inc(s_combt, 1)

            def split_high(n):
                high = blocks[n][0]
                b = stage_of[n]
                act.wait_ge(s_stage[b], 16 * (before[n] + 1))
                act.activation(high, stage[b][:, 0:high.shape[-1]], ACT.Copy).then_inc(s_split_hi, 1)

            def gate_silu(q, u):
                act.wait_ge(s_gate_ps, u + 1)
                if not isinstance(u, int) or u >= 2:
                    act.wait_ge(s_product, u - 1)
                act.activation(gate[:, q % 2, :], ps_gate[:, q % 2, :], ACT.Silu).then_inc(s_gate, 1)

            def hidden_high(q, u, hid_count):
                if q < ROUTED:
                    act.wait_ge(s_hid, hid_count + COMB_BUFS)
                else:
                    act.wait_ge(s_product, u + 1)
                act.wait_ge(s_down, u + 1)
                act.activation(hid_hi[:, hbuf_of(q), :], hid[:, q % 2, :], ACT.Copy).then_inc(s_hid_hi, 1)

            act.sem_inc(s_y_free, 1)
            for n in range(3):
                split_high(n)
            act.wait_ge(s_ident, 3)
            emb_out(0, ps_a, 1)
            emb_out(2, ps_c, 3)
            split_high(3)
            split_high(4)
            copy_out(xn_t[:, :], ps_a[:, :], s_xnt1_ps, 1, s_xnt1)
            copy_out(keyed_t[:, :], ps_b[:, :], s_key_ps, 1, s_key)
            split_high(5)
            copy_out(keyed_t[:, :], ps_a[:, :], s_got_ps, 1, s_got)
            split_high(6)
            copy_out(xn_t[:, :], ps_a[:, :], s_xnt2_ps, 1, s_xnt2)
            x_high(0, 1)
            split_high(7)
            exponents(1)
            split_high(8)
            comb_out(1)
            act.wait_ge(s_split_lo, len(blocks) - 1)
            for q in range(LEAD):
                gate_silu(q, q)
                if q < LEAD - 1:
                    hidden_high(q, q, q + 1)

            def sequence(i, more):
                nxt = held(act, (i + 1) % 2)
                tile0 = held(act, i * TILES)
                routed0 = held(act, i * ROUTED)
                for p in range(TILES):
                    if more and p == EMBED_T[0]:
                        emb_out(0, ps_a, i * NGRAMS + (NGRAMS + 1))
                    if more and p == EMBED_T[2]:
                        emb_out(2, ps_c, i * NGRAMS + 2 * NGRAMS)
                    if more and p == XNT_1:
                        copy_out(xn_t[:, :], ps_a[:, :], s_xnt1_ps, i + 2, s_xnt1)
                    if more and p == KEYED:
                        copy_out(keyed_t[:, :], ps_b[:, :], s_key_ps, i + 2, s_key)
                    if more and p == RETRIEVE:
                        copy_out(keyed_t[:, :], ps_a[:, :], s_got_ps, i + 2, s_got)
                    if more and p == XNT_2:
                        copy_out(xn_t[:, :], ps_a[:, :], s_xnt2_ps, i + 2, s_xnt2)
                    if more and p == XNT_2 + 1:
                        x_high(nxt, i + 2)
                    if more and p == COMB_T:
                        comb_out(i + 2)
                    if p == TILES - 1:
                        act.wait_ge(s_down, tile0 + (TILES + LEAD))
                        act.activation(y_t[:, :], ps_y[:, :], ACT.Copy).then_inc(s_y_free, 1)
                    if more or not tile_of(p)[0]:
                        gate_silu(tile_of(p)[1], tile0 + (p + LEAD))
                    if more and p == ROUTE + 3:
                        exponents(i + 2)
                    later, q = tile_of(p - 1)
                    if more or not later:
                        hidden_high(q, tile0 + (p + LEAD - 1), routed0 + (later * ROUTED + q + 1))

            with act.Fori(0, SEQS - 1) as i:
                sequence(i, True)
            sequence(SEQS - 1, False)

        @block.vector
        def _(dve):
            def modulo(dst, v, quotient, f, below_zero=False):
                dve.drain()
                dve.tensor_scalar(quotient, v, 1.0 / VOCAB, -0.5, ALU.mult, ALU.add)
                dve.drain()
                dve.scalar_tensor_tensor(out=dst, in0=quotient, scalar=-float(VOCAB), in1=v,
                                         op0=ALU.mult, op1=ALU.add)
                dve.drain()
                if below_zero:
                    dve.tensor_scalar(f, dst, 0.0, float(VOCAB), ALU.is_lt, ALU.mult)
                    dve.drain()
                    dve.tensor_tensor(dst, dst, f, ALU.add)
                    dve.drain()
                dve.tensor_scalar(f, dst, float(VOCAB), -float(VOCAB), ALU.is_ge, ALU.mult)
                dve.drain()
                dve.tensor_tensor(dst, dst, f, ALU.add)
                dve.drain()

            def roll(dst, hashed, token):
                n = dst.shape[-1]
                v = tmp_f[:, 1, 0:n]
                dve.scalar_tensor_tensor(out=v, in0=hashed, scalar=BASE, in1=token, op0=ALU.mult, op1=ALU.add)
                modulo(dst, v, tmp_i[:, 0:n], tmp_f[:, 0, 0:n])

            def split_low(n):
                high, low, _ = blocks[n]
                dve.wait_ge(s_split_hi, n + 1)
                dve.tensor_tensor(low, stage[stage_of[n]][:, 0:low.shape[-1]], high.bitcast(F32),
                                  ALU.subtract).then_inc(s_split_lo, 1)

            dve.sem_inc(s_hid, COMB_BUFS)
            dve.wait_ge(s_x, 48)
            dve.tensor_copy(xf[:, 0, :], xi[:, :])
            modulo(xf[:, 1, :], xf[:, 0, :], tmp_i[:, :], tmp_f[:, 0, :], below_zero=True)
            roll(xf[:, 2, 1:W], xf[:, 1, 0:W - 1], xf[:, 0, 1:W])
            dve.tensor_copy(id_f[:, 0, :], xf[:, 2, 2:P + 2]).then_inc(s_hash, 1)

            dve.wait_ge(s_spread_ps, 1)
            dve.tensor_copy(bias[:, :], ps_b[:, 0:P])
            dve.tensor_copy(scale[:, :], ps_b[:, P + 1:P + 2])
            dve.tensor_scalar(dcol[:, 1:2], ps_b[:, P:P + 1], -1.0, None, ALU.mult).then_inc(s_spread, 1)

            roll(xf[:, 3, 1:W - 1], xf[:, 2, 1:W - 1], xf[:, 0, 2:W])
            dve.tensor_copy(id_f[:, 1, :], xf[:, 3, 2:P + 2]).then_inc(s_hash, 1)

            def take_ids(n, ps):
                dve.wait_ge(s_hash_ps, n + 1)
                dve.tensor_copy(ids[:, n, 0:P], ps[:, 0:P]).then_inc(s_ids, 1)

            take_ids(0, ps_a)
            roll(tmp_f[:, 2, 2:W - 1], xf[:, 3, 1:W - 2], xf[:, 0, 3:W])
            dve.tensor_copy(id_f[:, 2, :], tmp_f[:, 2, 2:P + 2]).then_inc(s_hash, 1)
            take_ids(1, ps_c)
            take_ids(2, ps_y)

            dve.wait_ge(s_wt_ps, 1)
            dve.tensor_copy(w_t, ps_gate[:, 0, :].rearrange("p (a b) -> p a b", a=4)).then_inc(s_wt, 1)

            split_low(0)

            dve.memset(powers[:, :], 1.0)
            dve.wait_ge(s_const, 6)
            dve.wait_ge(s_pow, 1)
            dve.tensor_scalar(decay[:, :], dcol[:, 2:3], 1.0, None, ALU.add)
            dve.drain()
            dve.reciprocal(decay[:, :], decay[:, :])
            for b in range(7):
                dve.tensor_scalar(bit, exponent, b, 1, ALU.arith_shift_right, ALU.bitwise_and)
                dve.drain()
                dve.tensor_scalar(no_bit, bit, -1.0, 1.0, ALU.mult, ALU.add)
                dve.drain()
                dve.scalar_tensor_tensor(out=powers[:, :], in0=no_bit, scalar=decay[:, 0:1], in1=powers[:, :],
                                         op0=ALU.max, op1=ALU.mult)
                dve.drain()
                dve.tensor_tensor(decay[:, :], decay[:, :], decay[:, :], ALU.mult)
            dve.drain()
            dve.tensor_copy(decay_chunk[:, :], decay[:, :]).then_inc(s_power, 1)

            def emb_out(value):
                first, end = VALID[1]
                dve.wait_ge(s_emb_ps, value)
                dve.tensor_copy(emb_t[:, 1, first:end], ps_b[:, first:end]).then_inc(s_emb_dve, 1)

            def half_moments(t):
                dve.drain()
                for c in range(CHUNKS):
                    dve.bn_stats(out=stats[:, c, :], in_=t[:, c, :])

            def moments_of():
                dve.drain()
                for c in range(CHUNKS):
                    last = dve.bn_aggr(out=moments[:, c, :], in_=stats[:, c, :])
                last.then_inc(s_mom, 1)

            def embedded(k):
                dve.wait_ge(s_h1_ps, k)
                dve.tensor_tensor(h1[:, :, :], chunked(ps_b), bias[:, None, :].to_broadcast([P, CHUNKS, P]), ALU.add)

            def normalise(t, first, value):
                dve.wait_ge(s_rstd, value)
                for c in (first, first + 1):
                    last = dve.tensor_scalar(xn[:, c, :], t[:, c, :], moments[:, c, 0:1], rstd[:, c:c + 1],
                                             ALU.subtract, ALU.mult)
                if first:
                    last.then_inc(s_xn, 1)

            def key_decayed(k):
                dve.wait_ge(s_key, k)
                dve.tensor_tensor(keyed_out[:, :, :], chunked(keyed_t)[:, 0:CHUNKS - 1, :],
                                  decay_out[:, None, :].to_broadcast([P, CHUNKS - 1, P]),
                                  ALU.mult).then_inc(s_key_out, 1)

            def mask_scores(k):
                dve.wait_ge(s_score_ps, k)
                dve.tensor_tensor(scores[:, :, :], chunked(ps_a), decay_mask[:, None, :].to_broadcast([P, CHUNKS, P]),
                                  ALU.mult).then_inc(s_score, 1)

            def chain_states(k):
                dve.wait_ge(s_state_ps, k)
                last = dve.tensor_copy(state[:, CHUNKS - 2, :], ps_c[:, (CHUNKS - 2) * P:(CHUNKS - 1) * P])
                for j in range(CHUNKS - 3, -1, -1):
                    dve.drain()
                    last = dve.scalar_tensor_tensor(out=state[:, j, :], in0=state[:, j + 1, :],
                                                    scalar=decay_chunk[:, 0:1], in1=ps_c[:, j * P:(j + 1) * P],
                                                    op0=ALU.mult, op1=ALU.add)
                last.then_inc(s_state, 1)

            def half(t, par):
                return t[:, par, :].rearrange("p (c n) -> p c n", c=CHUNKS)

            def attended(par, k):
                dve.wait_ge(s_h2_ps, k)
                dve.tensor_tensor(half(h2, par), chunked(ps_b), h1[:, :, :], ALU.add)

            def take_logits(k):
                dve.wait_ge(s_route_ps, k)
                dve.tensor_copy(logits[:, :, :], ps_b[:, 0:CHUNKS * EXPERTS].rearrange("p (c e) -> p c e", c=CHUNKS))\
                   .then_inc(s_logits, 1)

            def sort_top():
                dve.drain()
                for c in range(CHUNKS):
                    dve.max(top[:, c, :], logits[:, c, :])

            def shift():
                dve.drain()
                dve.tensor_tensor(expo[:, :, :], logits[:, :, :],
                                  top[:, :, 0:1].to_broadcast([P, CHUNKS, EXPERTS]), ALU.subtract).then_inc(s_shift, 1)
                dve.memset(top[:, :, TOP_K:8], -HUGE)

            def strike_top():
                dve.drain()
                for c in range(CHUNKS):
                    dve.match_replace(out=struck[:, c, :], in_to_replace=top[:, c, :], in_values=logits[:, c, :],
                                      imm_value=-HUGE)

            def choose(k):
                dve.drain()
                dve.tensor_tensor(struck[:, :, :], struck[:, :, :], logits[:, :, :], ALU.not_equal)
                dve.drain()
                dve.wait_ge(s_exp, k)
                dve.tensor_tensor(struck[:, :, :], struck[:, :, :], expo[:, :, :], ALU.mult)

            def weigh():
                dve.drain()
                dve.tensor_reduce(total[:, :], struck[:, :, :], AX_X, ALU.add)
                dve.drain()
                dve.reciprocal(inv_total[:, :], total[:, :])
                dve.drain()
                dve.tensor_tensor(struck[:, :, :], struck[:, :, :],
                                  inv_total[:, :, None].to_broadcast([P, CHUNKS, EXPERTS]), ALU.mult).then_inc(s_comb, 1)

            def hidden(q, u, hid_count, spread_count):
                if not isinstance(u, int) or u >= 2:
                    dve.wait_ge(s_hid_lo, u - 1)
                dve.wait_ge(s_gate, u + 1)
                dve.wait_ge(s_lin_ps, u + 1)
                dst = product if q < ROUTED else hid
                dve.tensor_tensor(dst[:, q % 2, :], gate[:, q % 2, :], ps_lin[:, q % 2, :], ALU.mult).then_inc(s_product, 1)
                if q < ROUTED:
                    dve.drain()
                    dve.wait_ge(s_spread_w[q % COMB_BUFS], spread_count)
                    dve.tensor_tensor(hid[:, q % 2, :], product[:, q % 2, :], spread[:, q % COMB_BUFS, :],
                                      ALU.mult).then_inc(s_hid, 1)

            emb_out(2)
            dve.wait_ge(s_av_ps, 1)
            dve.tensor_copy(qk_w[:, :], ps_gate[:, 1, 0:P])
            dve.tensor_scalar(vo_w[:, :], ps_gate[:, 1, P:2 * P], scale[:, 0:1], None, ALU.mult).then_inc(s_av, 1)
            split_low(1)
            split_low(2)
            embedded(1)
            half_moments(h1)
            moments_of()
            split_low(3)
            normalise(h1, 0, 1)
            normalise(h1, 2, 1)
            split_low(4)
            chain_states(1)
            key_decayed(1)
            dve.wait_ge(s_pow, 2)
            mask_scores(1)
            split_low(5)
            attended(0, 1)
            half_moments(half(h2, 0))
            moments_of()
            split_low(6)
            normalise(half(h2, 0), 0, 2)
            normalise(half(h2, 0), 2, 2)
            take_logits(1)
            sort_top()
            shift()
            strike_top()
            choose(1)
            weigh()
            split_low(7)
            split_low(8)
            for q in range(LEAD):
                hidden(q, q, q + 1, 16)
            dve.sem_inc(s_res, 1)

            def sequence(i, more):
                cur = held(dve, i % 2)
                nxt = held(dve, (i + 1) % 2)
                tile0 = held(dve, i * TILES)
                routed0 = held(dve, i * ROUTED)
                spread0 = held(dve, i * (16 * ROUTED // COMB_BUFS))
                for p in range(TILES):
                    if more and p == EMBED_T[1]:
                        emb_out(i * NGRAMS + (NGRAMS + 2))
                    if more and p == EMBED_P:
                        embedded(i + 2)
                    if more and p == EMBED_P + 1:
                        half_moments(h1)
                    if more and p == EMBED_P + 2:
                        moments_of()
                    if more and p == EMBED_P + 3:
                        normalise(h1, 0, i * 2 + 3)
                    if more and p == EMBED_P + 4:
                        normalise(h1, 2, i * 2 + 3)
                    if more and p == STATE + 1:
                        chain_states(i + 2)
                    if more and p == KEYED + 1:
                        key_decayed(i + 2)
                    if more and p == SCORE + 1:
                        mask_scores(i + 2)
                    if more and p == PROJECT:
                        attended(nxt, i + 2)
                    if more and p == PROJECT + 1:
                        half_moments(half(h2, nxt))
                    if more and p == PROJECT + 2:
                        moments_of()
                    if more and p == PROJECT + 3:
                        normalise(half(h2, nxt), 0, i * 2 + 4)
                    if more and p == PROJECT + 4:
                        normalise(half(h2, nxt), 2, i * 2 + 4)
                    if more and p == ROUTE:
                        take_logits(i + 2)
                    if more and p == ROUTE + 1:
                        sort_top()
                    if more and p == ROUTE + 2:
                        shift()
                    if more and p == ROUTE + 3:
                        strike_top()
                    if more and p == ROUTE + 4:
                        choose(i + 2)
                    if more and p == ROUTE + 5:
                        weigh()
                    later, q = tile_of(p)
                    if more or not later:
                        hidden(q, tile0 + (p + LEAD), routed0 + (later * ROUTED + q + 1),
                               spread0 + 16 * ((later * ROUTED + q) // COMB_BUFS + 1))
                dve.wait_ge(s_res_ps, i + 1)
                dve.tensor_tensor(result[:, :, :], chunked(ps_c), half(h2, cur), ALU.add).then_inc(s_res, 1)

            with dve.Fori(0, SEQS - 1) as i:
                sequence(i, True)
            sequence(SEQS - 1, False)

        @block.tensor
        def _(pe):
            def chunk(t, c):
                return t[:, c * P:(c + 1) * P]

            def transposes(dst, parts, signal):
                for c, part in enumerate(parts):
                    last = pe.transpose(chunk(dst, c), part, ident[:, :])
                last.then_inc(signal, 1)

            pe.wait_ge(s_ident, 2)
            pe.wait_ge(s_row, 16)
            pe.matmul(ps_b[:, 0:P + 2], ones_row[:, :], row[:, :], start=True, stop=True).then_inc(s_spread_ps, 1)
            for n in range(NGRAMS):
                pe.wait_ge(s_hash, n + 1)
                transposes((ps_a, ps_c, ps_y)[n], [id_f[:, n, :]], s_hash_ps)
            pe.wait_ge(s_small, 64)
            for m in range(4):
                last = pe.matmul(ps_gate[:, 0, m * P:(m + 1) * P], small_w[:, 1 + m, :], small_w[:, 0, :],
                                 start=True, stop=True)
            last.then_inc(s_wt_ps, 1)

            def embed_t(n, gathered):
                pe.wait_ge(s_gath[n], gathered)
                transposes((ps_a, ps_b, ps_c)[n], [gath[:, n, c, :] for c in range(CHUNKS)], s_emb_ps)

            def embed_project():
                for c in range(CHUNKS):
                    for n in range(NGRAMS):
                        last = pe.matmul(chunk(ps_b, c), emb_t[:, n, c * P:(c + 1) * P], proj[:, n, :],
                                         start=(n == 0), stop=(n == NGRAMS - 1))
                last.then_inc(s_h1_ps, 1)

            def xn_transpose(value, signal):
                pe.wait_ge(s_xn, value)
                transposes(ps_a, [xn[:, c, :] for c in range(CHUNKS)], signal)

            def keyed(k):
                pe.wait_ge(s_xnt1, k)
                pe.matmul(ps_b[:, :], qk_w[:, :], xn_t[:, :], start=True, stop=True).then_inc(s_key_ps, 1)

            def score(k):
                pe.wait_ge(s_key, k)
                for c in range(CHUNKS):
                    last = pe.matmul(chunk(ps_a, c), chunk(xn_t, c), chunk(keyed_t, c), start=True, stop=True)
                last.then_inc(s_score_ps, 1)

            def chunk_sums(k):
                pe.wait_ge(s_xn_in, k)
                for j in range(CHUNKS - 1):
                    last = pe.matmul(chunk(ps_c, j), xn_in[:, j, :], xn[:, j + 1, :], start=True, stop=True)
                last.then_inc(s_state_ps, 1)

            def retrieve(k):
                pe.wait_ge(s_score, k)
                pe.wait_ge(s_state, k)
                pe.wait_ge(s_key_out, k)
                for c in range(CHUNKS):
                    last = pe.matmul(chunk(ps_a, c), xn[:, c, :], scores[:, c, :], start=True, stop=(c == CHUNKS - 1))
                    if c < CHUNKS - 1:
                        last = pe.matmul(chunk(ps_a, c), state[:, c, :], keyed_out[:, c, :], start=False, stop=True)
                last.then_inc(s_got_ps, 1)

            def project(k):
                pe.wait_ge(s_got, k)
                for c in range(CHUNKS):
                    last = pe.matmul(chunk(ps_b, c), chunk(keyed_t, c), vo_w[:, :], start=True, stop=True)
                last.then_inc(s_h2_ps, 1)

            def route(k):
                pe.wait_ge(s_xnt2, k)
                for c in range(CHUNKS):
                    last = pe.matmul(ps_b[:, c * EXPERTS:(c + 1) * EXPERTS], chunk(xn_t, c), wg[:, :],
                                     start=True, stop=True)
                last.then_inc(s_route_ps, 1)

            def comb_transpose(k):
                pe.wait_ge(s_comb, k)
                pe.sem_inc(steps["pe"], 1)
                for c in range(CHUNKS):
                    last = pe.transpose(chunk(ps_a, c)[0:EXPERTS, :], struck[:, c, :], ident[:, :])
                last.then_inc(s_combt_ps, 1)

            def up(q, par, u):
                cols = slice(q * P, (q + 1) * P)
                for m, (ps, used, signal) in enumerate(((ps_gate, s_gate, s_gate_ps), (ps_lin, s_product, s_lin_ps))):
                    if not isinstance(u, int) or u >= 2:
                        pe.wait_ge(used, u - 1)
                    dst = ps[:, q % 2, :]
                    pe.matmul(dst, up_hi[:, m, cols], x_hi[:, par, :], start=True, stop=False)
                    pe.matmul(dst, up_hi[:, m, cols], x_lo[:, par, :], start=False, stop=False)
                    pe.matmul(dst, up_lo[:, m, cols], x_hi[:, par, :], start=False, stop=True).then_inc(signal, 1)

            def down_tile(q, u):
                cols = slice(q * P, (q + 1) * P)
                pe.wait_ge(s_hid_lo, u + 1)
                pe.matmul(ps_y[:, :], down_hi[:, cols], hid_hi[:, hbuf_of(q), :], start=(q == 0), stop=False)
                pe.matmul(ps_y[:, :], down_hi[:, cols], hid_lo[:, hbuf_of(q), :], start=False, stop=False)
                pe.matmul(ps_y[:, :], down_lo[:, cols], hid_hi[:, hbuf_of(q), :], start=False,
                          stop=(q == TILES - 1)).then_inc(s_down, 1)

            embed_t(0, 16 * CHUNKS)
            pe.wait_ge(s_spread, 1)
            embed_t(1, 16 * CHUNKS)
            embed_t(2, 16 * CHUNKS)
            pe.wait_ge(s_wt, 1)
            for m in range(2):
                last = pe.matmul(ps_gate[:, 1, m * P:(m + 1) * P], w_t[:, 2 * m, :], w_t[:, 2 * m + 1, :],
                                 start=True, stop=True)
            last.then_inc(s_av_ps, 1)
            pe.wait_ge(s_emb_act, 2)
            pe.wait_ge(s_emb_dve, 1)
            embed_project()
            xn_transpose(1, s_xnt1_ps)
            pe.wait_ge(s_av, 1)
            keyed(1)
            chunk_sums(1)
            score(1)
            retrieve(1)
            project(1)
            xn_transpose(2, s_xnt2_ps)
            route(1)
            comb_transpose(1)
            pe.wait_ge(s_split_lo, 2)
            pe.wait_ge(s_x_lo, 1)
            pe.sem_inc(s_down, LEAD)
            for q in range(LEAD):
                up(q, 0, q)

            def sequence(i, more):
                cur = held(pe, i % 2)
                nxt = held(pe, (i + 1) % 2)
                tile0 = held(pe, i * TILES)
                for p in range(TILES):
                    if more and p == EMBED_T[0]:
                        pe.wait_ge(s_combt, i + 1)
                        embed_t(0, i * (16 * CHUNKS) + 2 * 16 * CHUNKS)
                    if more and p == EMBED_T[1]:
                        pe.wait_ge(s_logits, i + 1)
                        embed_t(1, i * (16 * CHUNKS) + 2 * 16 * CHUNKS)
                    if more and p == EMBED_T[2]:
                        pe.wait_ge(s_res, i + 1)
                        embed_t(2, i * (16 * CHUNKS) + 2 * 16 * CHUNKS)
                    if more and p == EMBED_P:
                        pe.wait_ge(s_emb_act, i * 2 + 4)
                        pe.wait_ge(s_emb_dve, i + 2)
                        embed_project()
                    if more and p == XNT_1:
                        xn_transpose(i * 2 + 3, s_xnt1_ps)
                    if more and p == KEYED:
                        keyed(i + 2)
                    if more and p == STATE:
                        chunk_sums(i + 2)
                    if more and p == SCORE:
                        score(i + 2)
                    if more and p == RETRIEVE:
                        retrieve(i + 2)
                    if more and p == PROJECT:
                        project(i + 2)
                    if more and p == XNT_2:
                        xn_transpose(i * 2 + 4, s_xnt2_ps)
                    if more and p == ROUTE:
                        route(i + 2)
                    if more and p == COMB_T:
                        comb_transpose(i + 2)
                    if p == 0:
                        pe.wait_ge(s_y_free, i + 1)
                    later, q = tile_of(p)
                    if p == TILES - 1:
                        down_tile(p, tile0 + p)
                    if more and later and q == 0:
                        pe.wait_ge(s_x_lo, i + 2)
                    if more or not later:
                        up(q, nxt if later else cur, tile0 + (p + LEAD))
                    if p < TILES - 1:
                        down_tile(p, tile0 + p)
                pe.wait_ge(s_y_free, i + 2)
                transposes(ps_c, [chunk(y_t, c) for c in range(CHUNKS)], s_res_ps)

            with pe.Fori(0, SEQS - 1) as i:
                sequence(i, True)
            sequence(SEQS - 1, False)


def kernel(**inputs):
    import concourse.bacc as bacc
    from concourse.bass_utils import run_bass_kernel_spmd

    nc = bacc.Bacc("TRN2", target_bir_lowering=False, num_devices=1)
    a = {k: np.asarray(v) for k, v in inputs.items()}

    def interleaved(name):
        return a[name].reshape(ROUTED, 2, INTER, P).transpose(0, 2, 1, 3).reshape(EXPERTS * INTER, P)

    def hidden_major(name, shared):
        return np.concatenate([interleaved(name), a[shared]], axis=0).T

    down = np.concatenate([interleaved("L0_ffn_w2"), a["L0_ffn_w_sd"].T], axis=0)
    arrays = {
        "x": a["x"].reshape(P, P),
        "emb_2": a["L0_tok_emb_2"], "emb_3": a["L0_tok_emb_3"], "emb_4": a["L0_tok_emb_4"],
        "proj_t": a["L0_tok_proj_w"].T.reshape(NGRAMS, P, P).transpose(1, 0, 2),
        "rows": np.concatenate([a["L0_tok_proj_b"].reshape(1, P), a["L0_attn_decay_logit"].reshape(1, 1),
                                a["L0_attn_out_scale"].reshape(1, 1)], axis=1),
        "basis_t": a["L0_attn_basis"].T,
        "coeff_t": np.stack([a[f"L0_attn_{m}_coeffs"].T for m in "qkvo"], axis=1),
        "wg_t": a["L0_ffn_w_gate"].T,
        "up_gate": hidden_major("L0_ffn_w1", "L0_ffn_w_sg"),
        "up_lin": hidden_major("L0_ffn_w3", "L0_ffn_w_su"),
        "down": down.reshape(TILES, P, P).transpose(1, 0, 2).reshape(P, TILES * P),
    }
    arrays = {k: np.ascontiguousarray(v) for k, v in arrays.items()}
    ap = {k: nc.dram_tensor(k, v.shape, mybir.dt.from_np(v.dtype), kind="ExternalInput").ap()
          for k, v in arrays.items()}
    out = nc.dram_tensor("out", (SEQS, SEQ_LEN, P), F32, kind="ExternalOutput").ap()
    comb_dram = nc.dram_tensor("comb_dram", (2, EXPERTS, SEQ_LEN), F32, kind="Internal").ap()
    build(nc, ap["x"], [ap["emb_2"], ap["emb_3"], ap["emb_4"]], ap["proj_t"], ap["rows"], ap["basis_t"],
          ap["coeff_t"], ap["wg_t"], ap["up_gate"], ap["up_lin"], ap["down"],
          comb_dram, out.rearrange("s (c p) d -> s p c d", c=CHUNKS))
    return run_bass_kernel_spmd(nc, [arrays], core_ids=[0]).results[0]["out"]
```
